# Optimizing a Trainium2 kernel written in Bass

```python
import numpy as np
import jax
import jax.numpy as jnp

def _softmax(x, axis=-1):
    return jax.nn.softmax(x, axis=axis)

def _gelu(x):
    return jax.nn.gelu(x, approximate=True)

def _silu(x):
    return jax.nn.silu(x)

def _sigmoid(x):
    return jax.nn.sigmoid(x)

def _layernorm(x, axis=-1, eps=1e-05):
    m = jnp.mean(x, axis=axis, keepdims=True)
    v = jnp.var(x, axis=axis, keepdims=True)
    return (x - m) / jnp.sqrt(v + eps)

def _scatter_add(tgt, idx, src, axis=0):
    return tgt.at[idx].add(src)

def _segment_sum(src, seg, n):
    return jax.ops.segment_sum(src, seg, n)
kernel_name = 'mk_dlrm_tower_d1_rec_r8_6b3d88'

def setup_inputs(seed: int=0):
    np.random.seed(seed)
    _w = jnp.asarray

    def _rec_inputs():
        import jax
        import jax.numpy as jnp
        _tk = jax.random.key(seed)
        ids = jnp.stack([jax.random.randint(jax.random.fold_in(_tk, 200 + f), (512,), 0, v, jnp.int32) for f, v in enumerate([125000, 1000, 12500, 1250, 1250, 1000, 1000, 1000, 1250, 1250, 1250, 1000, 1000, 12500, 1000, 1000, 1250, 1250, 12500, 12500, 12500, 12500, 1000, 1000, 1000, 1000])], axis=1)
        tbl_0 = 0.05 * jax.random.normal(jax.random.fold_in(_tk, 500 + 0), (125000, 128), jnp.float32)
        tbl_1 = 0.05 * jax.random.normal(jax.random.fold_in(_tk, 500 + 1), (1000, 128), jnp.float32)
        tbl_2 = 0.05 * jax.random.normal(jax.random.fold_in(_tk, 500 + 2), (12500, 128), jnp.float32)
        tbl_3 = 0.05 * jax.random.normal(jax.random.fold_in(_tk, 500 + 3), (1250, 128), jnp.float32)
        tbl_4 = 0.05 * jax.random.normal(jax.random.fold_in(_tk, 500 + 4), (1250, 128), jnp.float32)
        tbl_5 = 0.05 * jax.random.normal(jax.random.fold_in(_tk, 500 + 5), (1000, 128), jnp.float32)
        tbl_6 = 0.05 * jax.random.normal(jax.random.fold_in(_tk, 500 + 6), (1000, 128), jnp.float32)
        tbl_7 = 0.05 * jax.random.normal(jax.random.fold_in(_tk, 500 + 7), (1000, 128), jnp.float32)
        tbl_8 = 0.05 * jax.random.normal(jax.random.fold_in(_tk, 500 + 8), (1250, 128), jnp.float32)
        tbl_9 = 0.05 * jax.random.normal(jax.random.fold_in(_tk, 500 + 9), (1250, 128), jnp.float32)
        tbl_10 = 0.05 * jax.random.normal(jax.random.fold_in(_tk, 500 + 10), (1250, 128), jnp.float32)
        tbl_11 = 0.05 * jax.random.normal(jax.random.fold_in(_tk, 500 + 11), (1000, 128), jnp.float32)
        tbl_12 = 0.05 * jax.random.normal(jax.random.fold_in(_tk, 500 + 12), (1000, 128), jnp.float32)
        tbl_13 = 0.05 * jax.random.normal(jax.random.fold_in(_tk, 500 + 13), (12500, 128), jnp.float32)
        tbl_14 = 0.05 * jax.random.normal(jax.random.fold_in(_tk, 500 + 14), (1000, 128), jnp.float32)
        tbl_15 = 0.05 * jax.random.normal(jax.random.fold_in(_tk, 500 + 15), (1000, 128), jnp.float32)
        tbl_16 = 0.05 * jax.random.normal(jax.random.fold_in(_tk, 500 + 16), (1250, 128), jnp.float32)
        tbl_17 = 0.05 * jax.random.normal(jax.random.fold_in(_tk, 500 + 17), (1250, 128), jnp.float32)
        tbl_18 = 0.05 * jax.random.normal(jax.random.fold_in(_tk, 500 + 18), (12500, 128), jnp.float32)
        tbl_19 = 0.05 * jax.random.normal(jax.random.fold_in(_tk, 500 + 19), (12500, 128), jnp.float32)
        tbl_20 = 0.05 * jax.random.normal(jax.random.fold_in(_tk, 500 + 20), (12500, 128), jnp.float32)
        tbl_21 = 0.05 * jax.random.normal(jax.random.fold_in(_tk, 500 + 21), (12500, 128), jnp.float32)
        tbl_22 = 0.05 * jax.random.normal(jax.random.fold_in(_tk, 500 + 22), (1000, 128), jnp.float32)
        tbl_23 = 0.05 * jax.random.normal(jax.random.fold_in(_tk, 500 + 23), (1000, 128), jnp.float32)
        tbl_24 = 0.05 * jax.random.normal(jax.random.fold_in(_tk, 500 + 24), (1000, 128), jnp.float32)
        tbl_25 = 0.05 * jax.random.normal(jax.random.fold_in(_tk, 500 + 25), (1000, 128), jnp.float32)
        _rk = jax.random.fold_in(_tk, 7)
        r_dense_features = 7.22013e-05 + 1.00017 * jax.random.normal(jax.random.fold_in(_rk, 101), (512, 128), jnp.float32)
        W_top1 = 0.0456912 * jax.random.normal(jax.random.fold_in(_tk, 801), (479, 512), jnp.float32)
        W_top2 = 0.0441942 * jax.random.normal(jax.random.fold_in(_tk, 802), (512, 256), jnp.float32)
        W_top3 = 0.0625 * jax.random.normal(jax.random.fold_in(_tk, 803), (256, 1), jnp.float32)
        b_top1 = jnp.zeros((512,), jnp.float32)
        b_top2 = jnp.zeros((256,), jnp.float32)
        return (r_dense_features, ids, tbl_0, tbl_1, tbl_2, tbl_3, tbl_4, tbl_5, tbl_6, tbl_7, tbl_8, tbl_9, tbl_10, tbl_11, tbl_12, tbl_13, tbl_14, tbl_15, tbl_16, tbl_17, tbl_18, tbl_19, tbl_20, tbl_21, tbl_22, tbl_23, tbl_24, tbl_25, W_top1, b_top1, W_top2, b_top2, W_top3)
    r_dense_features, ids, tbl_0, tbl_1, tbl_2, tbl_3, tbl_4, tbl_5, tbl_6, tbl_7, tbl_8, tbl_9, tbl_10, tbl_11, tbl_12, tbl_13, tbl_14, tbl_15, tbl_16, tbl_17, tbl_18, tbl_19, tbl_20, tbl_21, tbl_22, tbl_23, tbl_24, tbl_25, W_top1, b_top1, W_top2, b_top2, W_top3 = _rec_inputs()

    def _L0_rec_setup():
        import jax, jax.numpy as jnp
        import numpy as np
        FEATURE_NUM = 27
        key = jax.random.key(seed)
        k1, k2 = jax.random.split(key)
        B, N, D = (8192, FEATURE_NUM - 1, 128)
        dense_features = jax.random.normal(k1, (B, D), dtype=jnp.float32)
        sparse_features = jax.random.normal(k2, (B, N, D), dtype=jnp.float32)
        return {'dense_features': dense_features, 'sparse_features': sparse_features}
    _L0_rec_all = _L0_rec_setup()
    _L0_rec_in = {k: v for k, v in _L0_rec_all.items() if k in ()}
    del _L0_rec_all
    return {'r_dense_features': r_dense_features, 'ids': ids, 'tbl_0': tbl_0, 'tbl_1': tbl_1, 'tbl_2': tbl_2, 'tbl_3': tbl_3, 'tbl_4': tbl_4, 'tbl_5': tbl_5, 'tbl_6': tbl_6, 'tbl_7': tbl_7, 'tbl_8': tbl_8, 'tbl_9': tbl_9, 'tbl_10': tbl_10, 'tbl_11': tbl_11, 'tbl_12': tbl_12, 'tbl_13': tbl_13, 'tbl_14': tbl_14, 'tbl_15': tbl_15, 'tbl_16': tbl_16, 'tbl_17': tbl_17, 'tbl_18': tbl_18, 'tbl_19': tbl_19, 'tbl_20': tbl_20, 'tbl_21': tbl_21, 'tbl_22': tbl_22, 'tbl_23': tbl_23, 'tbl_24': tbl_24, 'tbl_25': tbl_25, 'W_top1': W_top1, 'b_top1': b_top1, 'W_top2': W_top2, 'b_top2': b_top2, 'W_top3': W_top3}

def reference(r_dense_features, ids, tbl_0, tbl_1, tbl_2, tbl_3, tbl_4, tbl_5, tbl_6, tbl_7, tbl_8, tbl_9, tbl_10, tbl_11, tbl_12, tbl_13, tbl_14, tbl_15, tbl_16, tbl_17, tbl_18, tbl_19, tbl_20, tbl_21, tbl_22, tbl_23, tbl_24, tbl_25, W_top1, b_top1, W_top2, b_top2, W_top3):
    import jax
    import jax.numpy as jnp

    def _L0_rec_ref(dense_features, sparse_features):
        import jax, jax.numpy as jnp
        import numpy as np
        FEATURE_NUM = 27
        combined = jnp.concatenate([dense_features[:, None, :], sparse_features], axis=1)
        interactions = jnp.einsum('bfd,bgd->bfg', combined, combined)
        iu, ju = jnp.triu_indices(FEATURE_NUM, k=1)
        return interactions[:, iu, ju]
    e = jnp.stack([tbl_0[ids[:, 0]], tbl_1[ids[:, 1]], tbl_2[ids[:, 2]], tbl_3[ids[:, 3]], tbl_4[ids[:, 4]], tbl_5[ids[:, 5]], tbl_6[ids[:, 6]], tbl_7[ids[:, 7]], tbl_8[ids[:, 8]], tbl_9[ids[:, 9]], tbl_10[ids[:, 10]], tbl_11[ids[:, 11]], tbl_12[ids[:, 12]], tbl_13[ids[:, 13]], tbl_14[ids[:, 14]], tbl_15[ids[:, 15]], tbl_16[ids[:, 16]], tbl_17[ids[:, 17]], tbl_18[ids[:, 18]], tbl_19[ids[:, 19]], tbl_20[ids[:, 20]], tbl_21[ids[:, 21]], tbl_22[ids[:, 22]], tbl_23[ids[:, 23]], tbl_24[ids[:, 24]], tbl_25[ids[:, 25]]], axis=1)
    z = _L0_rec_ref(r_dense_features, e)
    z = z.reshape(z.shape[0], -1)
    h = jnp.concatenate([z, r_dense_features], axis=1)
    h = jnp.maximum(h @ W_top1 + b_top1, 0.0)
    h = jnp.maximum(h @ W_top2 + b_top2, 0.0)
    y = h @ W_top3
    return y

_drawn_inputs = setup_inputs


def setup_inputs(seed=0):
    import zlib

    import numpy as np

    out = dict(_drawn_inputs(seed))
    spreads = {'b_top1': (0.0, 0.1), 'b_top2': (0.0, 0.1)}
    factors = {}
    for name, (base, spread) in spreads.items():
        noise = np.random.default_rng([zlib.crc32(name.encode()), seed]).standard_normal(out[name].shape)
        drawn = base * np.exp(spread * noise) if base else spread * noise
        out[name] = jnp.asarray(drawn.astype(out[name].dtype))
    for name, factor in factors.items():
        out[name] = (out[name] * factor).astype(out[name].dtype)
    return out
```

```python
import concourse.bass as bass
from concourse import mybir
from contextlib import ExitStack

N_TABLES = 26
CHUNKS = 8
SELECTED = 7


def dlrm_tower_kernel(nc, ids, ids_rows, dense, sel_tables, tables, w1, b1, w2, b2, w3, out):
    f32, f32r, i32 = mybir.dt.float32, mybir.dt.float32r, mybir.dt.int32
    ACT, ALU = mybir.ActivationFunctionType, mybir.AluOpType

    P = 128
    T = ids.shape[1]
    S = len(sel_tables)
    F = S + 1 + len(tables)
    M = F - S
    RP = sel_tables[0].shape[0] // CHUNKS
    G = F - 1
    Q = 4
    SLOT = 32
    SB = P // Q
    HB = SB // 2
    NK = -(-G // Q)
    NG = -(-M // Q)
    H1, H2 = w1.shape[2], w2.shape[1]
    C1, C2 = H1 // P, H2 // P

    TB = 3
    OB = 4

    def group(q):
        return range(Q * q, min(Q * q + Q, M))

    with ExitStack() as ctx:
        def sb(name, shape, dt=f32):
            return ctx.enter_context(nc.sbuf_tensor(name, shape, dt))

        def ps(name, shape):
            return ctx.enter_context(nc.psum_tensor(name, shape, f32))

        def sem(name):
            return ctx.enter_context(nc.semaphore(name))

        ids_sb = sb("ids_sb", [P, T, M - 1], i32)
        ident = sb("ident", [P, P])
        rows = sb("rows", [P, T, M, P])
        feats = sb("feats", [P, T, SB, Q, SLOT])
        ids_bc = [sb(f"ids_bc{i}", [RP, T * P], i32) for i in range(TB)]
        tab = [sb(f"tab{i}", [RP, CHUNKS, P]) for i in range(TB)]
        tab_hi = [sb(f"tab_hi{i}", [RP, CHUNKS, P], f32r) for i in range(2)]
        tab_lo = [sb(f"tab_lo{i}", [RP, CHUNKS, P], f32r) for i in range(2)]
        onehot = [sb(f"onehot{i}", [RP, T * P], f32r) for i in range(OB)]
        row_of_i = sb("row_of_i", [RP, CHUNKS], i32)
        row_of = sb("row_of", [RP, CHUNKS])
        denseT = [sb(f"denseT{i}", [P, P]) for i in range(2)]
        pairs = [sb(f"pairs{i}", [P, NK, P]) for i in range(2)]
        w1_sb = sb("w1_sb", [P, NK + 1, H1])
        w2_sb = sb("w2_sb", [P, C1, H2])
        w3_sb = sb("w3_sb", [P, C2])
        b1_sb = sb("b1_sb", [P, C1])
        b2_sb = sb("b2_sb", [P, C2])
        h1 = [sb(f"h1_{i}", [P, C1, P]) for i in range(2)]
        h2 = [sb(f"h2_{i}", [P, C2, P]) for i in range(2)]
        y = sb("y", [1, T * P])

        tr_ps = [ps(f"tr_ps{i}", [P, Q, P]) for i in range(2)]
        gram_ps = ps("gram_ps", [P, HB, P])
        mlp_ps = [ps(f"mlp_ps{i}", [P, Q, P]) for i in range(2)]

        ids_loaded = sem("ids_loaded")
        small_loaded = sem("small_loaded")
        w1_loaded = sem("w1_loaded")
        w2_loaded = sem("w2_loaded")
        dense_loaded = sem("dense_loaded")
        gathered = [[sem(f"gathered{t}_{q}") for q in range(NG)] for t in range(T)]
        ids_bc_loaded = [sem(f"ids_bc_loaded{i}") for i in range(TB)]
        tab_loaded = [sem(f"tab_loaded{i}") for i in range(TB)]
        row_numbers = sem("row_numbers")
        hi_ready = sem("hi_ready")
        lo_ready = sem("lo_ready")
        onehot_ready = sem("onehot_ready")
        onehot_used = sem("onehot_used")
        selected_copied = sem("selected_copied")
        zeroed = sem("zeroed")
        ident_ready = sem("ident_ready")
        pads_ready = sem("pads_ready")
        transposed = sem("transposed")
        feats_by_act = sem("feats_by_act")
        feats_by_dve = sem("feats_by_dve")
        dense_copied = sem("dense_copied")
        gram_done = sem("gram_done")
        pairs_by_act = sem("pairs_by_act")
        pairs_by_dve = sem("pairs_by_dve")
        layer1_done = sem("layer1_done")
        h1_by_act = sem("h1_by_act")
        h1_by_dve = sem("h1_by_dve")
        layer2_done = sem("layer2_done")
        h2_by_act = sem("h2_by_act")
        h2_by_dve = sem("h2_by_dve")
        layer3_done = sem("layer3_done")
        y_ready = sem("y_ready")
        stored = sem("stored")

        def by_act(n):
            return n < NG or n % 2 == 0

        def act_groups(n):
            return len([m for m in range(n) if by_act(m)])

        def dve_groups(n):
            return n - act_groups(n)

        block = ctx.enter_context(nc.Block())

        @block.sync
        def _(sp):
            sp.dma_start(ids_sb[:], ids).then_inc(ids_loaded, 16)
            for i in range(S):
                if i >= TB:
                    sp.wait_ge(onehot_ready, CHUNKS * (i - TB + 1))
                    sp.wait_ge(lo_ready, i - TB + 1)
                sp.dma_start(ids_bc[i % TB][:], ids_rows[i, :].partition_broadcast(RP)).then_inc(
                    ids_bc_loaded[i % TB], 16)
                sp.dma_start(tab[i % TB][:], sel_tables[i].rearrange("(p c) d -> p c d", c=CHUNKS)).then_inc(
                    tab_loaded[i % TB], 16)
                if i == 0:
                    sp.dma_start(rows[:, :, 0, :], dense.rearrange("(t p) d -> p t d", p=P)).then_inc(
                        dense_loaded, 16)
            sp.dma_start(w1_sb[:], w1).then_inc(w1_loaded, 16)
            sp.dma_start(w2_sb[:], w2.rearrange("(c p) n -> p c n", p=P)).then_inc(w2_loaded, 16)
            sp.dma_start(b1_sb[:], b1).then_inc(small_loaded, 16)
            sp.dma_start(b2_sb[:], b2).then_inc(small_loaded, 16)
            sp.dma_start(w3_sb[:], w3).then_inc(small_loaded, 16)
            sp.wait_ge(y_ready, T)
            sp.dma_start(out, y[:]).then_inc(stored, 16)
            sp.wait_ge(stored, 16)

        @block.gpsimd
        def _(pool):
            nc.gpsimd.memset(ident[:], 0.0).then_inc(zeroed, 1)
            pool.wait_ge(zeroed, 1)
            nc.gpsimd.affine_select(out=ident[:], in_=ident[:], compare_op=ALU.not_equal, fill=1.0, base=0,
                                    pattern=[[-1, P]], channel_multiplier=1).then_inc(ident_ready, 1)
            nc.gpsimd.iota(row_of_i[:], pattern=[[1, CHUNKS]], base=0, channel_multiplier=CHUNKS).then_inc(
                row_numbers, 1)
            pool.wait_ge(ids_loaded, 16)
            for t in range(T):
                for m in range(1, M):
                    nc.gpsimd.indirect_dma_start(
                        out=rows[:, t, m, :], out_offset=None, in_=tables[m - 1],
                        in_offset=bass.IndirectOffsetOnAxis(ap=ids_sb[:, t, m - 1:m], axis=0),
                    ).then_inc(gathered[t][m // Q], 16)

        @block.tensor
        def _(pe):
            def select(i):
                pe.wait_ge(hi_ready, i + 1)
                pe.wait_ge(lo_ready, i + 1)
                if i >= 2:
                    pe.wait_ge(selected_copied, i - 1)
                bank = gram_ps[:, Q * (i % 2):Q * (i % 2 + 1), :].rearrange("p a b -> p (a b)")
                for c in range(CHUNKS):
                    o = CHUNKS * i + c
                    pe.wait_ge(onehot_ready, o + 1)
                    nc.tensor.matmul(bank, tab_hi[i % 2][:, c, :], onehot[o % OB][:], start=(c == 0), stop=False)
                    nc.tensor.matmul(bank, tab_lo[i % 2][:, c, :], onehot[o % OB][:], start=False,
                                     stop=(c == CHUNKS - 1)).then_inc(onehot_used, 1)

            def transpose_group(t, q):
                n = NG * t + q
                if q == 0:
                    pe.wait_ge(dense_loaded, 16)
                pe.wait_ge(gathered[t][q], 16 * len([m for m in group(q) if m]))
                if n >= 2:
                    if (n - 2) % NG == 0:
                        pe.wait_ge(dense_copied, (n - 2) // NG + 1)
                    if by_act(n - 2):
                        pe.wait_ge(feats_by_act, act_groups(n - 1))
                    else:
                        pe.wait_ge(feats_by_dve, dve_groups(n - 1))
                for c, m in enumerate(group(q)):
                    last = nc.tensor.transpose(tr_ps[n % 2][:, c, :], rows[:, t, m, :], ident[:])
                last.then_inc(transposed, 1)

            def gram(t, h):
                u = 2 * t + h
                if u == 0:
                    pe.wait_ge(pads_ready, 1)
                    pe.wait_ge(selected_copied, S)
                if h == 0:
                    pe.wait_ge(feats_by_act, act_groups(NG * (t + 1)))
                    if t >= 1:
                        pe.wait_ge(feats_by_dve, dve_groups(NG * (t + 1)))
                if u >= 1:
                    pe.wait_ge(pairs_by_act, u)
                    pe.wait_ge(pairs_by_dve, u)
                for i in range(HB):
                    x = feats[:, t, HB * h + i, :, :]
                    last = nc.tensor.matmul(gram_ps[:, i, 0:Q * G], x.rearrange("p s f -> p (s f)"),
                                            x[:, :, 1:F], start=True, stop=True)
                last.then_inc(gram_done, 1)

            def layer1(t):
                if t == 0:
                    pe.wait_ge(w1_loaded, 16)
                else:
                    pe.wait_ge(y_ready, t)
                    pe.wait_ge(h2_by_dve, t)
                pe.wait_ge(pairs_by_act, 2 * (t + 1))
                pe.wait_ge(pairs_by_dve, 2 * (t + 1))
                pe.wait_ge(dense_copied, t + 1)
                for c in range(C1):
                    nc.tensor.matmul(mlp_ps[c // 2][:, c % 2, :], w1_sb[:, NK, P * c:P * (c + 1)], denseT[t % 2][:],
                                     start=True, stop=False)
                    for k in range(NK):
                        last = nc.tensor.matmul(mlp_ps[c // 2][:, c % 2, :], w1_sb[:, k, P * c:P * (c + 1)],
                                                pairs[t % 2][:, k, :], start=False, stop=(k == NK - 1))
                    if c % 2 == 1:
                        last.then_inc(layer1_done, 1)

            def layer2(t):
                if t == 0:
                    pe.wait_ge(w2_loaded, 16)
                for e in range(C2):
                    for c in range(C1):
                        if e == 0 and c == 0:
                            pe.wait_ge(h1_by_act, t + 1)
                        if e == 0 and c == C1 // 2:
                            pe.wait_ge(h1_by_dve, t + 1)
                        last = nc.tensor.matmul(mlp_ps[e][:, 2, :], w2_sb[:, c, P * e:P * (e + 1)], h1[t % 2][:, c, :],
                                                start=(c == 0), stop=(c == C1 - 1))
                    last.then_inc(layer2_done, 1)

            def layer3(t):
                if t == 0:
                    pe.wait_ge(small_loaded, 48)
                for e in range(C2):
                    if e == 0:
                        pe.wait_ge(h2_by_act, t + 1)
                    else:
                        pe.wait_ge(h2_by_dve, t + 1)
                    last = nc.tensor.matmul(mlp_ps[0][0:1, 3, :], w3_sb[:, e:e + 1], h2[t % 2][:, e, :],
                                            start=(e == 0), stop=(e == C2 - 1))
                last.then_inc(layer3_done, 1)

            pe.wait_ge(ident_ready, 1)
            for i in range(S):
                select(i)
                if i >= 1 and i - 1 < NG:
                    transpose_group(0, i - 1)
            for q in range(max(S - 1, 0), NG):
                transpose_group(0, q)
            for t in range(T):
                gram(t, 0)
                if t == 0:
                    transpose_group(1, 0)
                    transpose_group(1, 1)
                else:
                    layer1(t - 1)
                gram(t, 1)
                if t > 0:
                    layer2(t - 1)
                    layer3(t - 1)
                if t + 1 < T:
                    for q in range(2 if t == 0 else 0, NG):
                        transpose_group(t + 1, q)
            layer1(T - 1)
            layer2(T - 1)
            layer3(T - 1)

        def feats_views(t, q):
            n = NG * t + q
            w = len(group(q))
            src = tr_ps[n % 2][:, 0:w, :].rearrange("p f (s i) -> p s i f", s=Q)
            dst = feats[:, t, :, :, S + Q * q:S + Q * q + w].rearrange("p i s f -> p s i f")
            return src, dst

        def pairs_views(t, h, s, j):
            nk = len(range(j, G, Q))
            src = gram_ps[SLOT * s:SLOT * (s + 1), :, G * s + j:G * (s + 1):Q].rearrange("p i k -> p k i")
            dst = pairs[t % 2][SLOT * j:SLOT * (j + 1), 0:nk, SB * s + HB * h:SB * s + HB * (h + 1)]
            return src, dst

        @block.scalar
        def _(act):
            def make_hi(i):
                act.wait_ge(tab_loaded[i % TB], 16 * (i // TB + 1))
                if i >= 2:
                    act.wait_ge(onehot_used, CHUNKS * (i - 1))
                nc.scalar.activation(tab_hi[i % 2][:], tab[i % TB][:], ACT.Copy).then_inc(hi_ready, 1)

            def copy_selected(i):
                act.wait_ge(onehot_used, CHUNKS * (i + 1))
                src = gram_ps[:, Q * (i % 2):Q * (i % 2 + 1), :].rearrange("p t (s i) -> p t s i", s=Q)
                dst = feats[:, :, :, :, i].rearrange("p t i s -> p t s i")
                nc.scalar.activation(dst, src, ACT.Copy).then_inc(selected_copied, 1)

            def copy_group(t, q):
                n = NG * t + q
                if not by_act(n):
                    return
                act.wait_ge(transposed, n + 1)
                if q == 0:
                    if t >= 2:
                        act.wait_ge(layer1_done, 2 * (t - 1))
                    nc.scalar.activation(denseT[t % 2][:], tr_ps[n % 2][:, 0, :], ACT.Copy).then_inc(dense_copied, 1)
                src, dst = feats_views(t, q)
                nc.scalar.activation(dst, src, ACT.Copy).then_inc(feats_by_act, 1)

            def copy_pairs(t, h):
                act.wait_ge(gram_done, 2 * t + h + 1)
                if t >= 2:
                    act.wait_ge(layer1_done, 2 * (t - 1))
                for s in (2, 3):
                    for j in range(Q):
                        src, dst = pairs_views(t, h, s, j)
                        last = nc.scalar.activation(dst, src, ACT.Copy)
                last.then_inc(pairs_by_act, 1)

            def relu1(t):
                if t == 0:
                    act.wait_ge(small_loaded, 48)
                if t >= 2:
                    act.wait_ge(layer2_done, C2 * (t - 1))
                act.wait_ge(layer1_done, 2 * t + 1)
                for c in (0, 1):
                    last = nc.scalar.activation(h1[t % 2][:, c, :], mlp_ps[0][:, c, :], ACT.Relu,
                                                bias=b1_sb[:, c:c + 1])
                last.then_inc(h1_by_act, 1)

            def relu2(t):
                act.wait_ge(layer2_done, C2 * t + 1)
                if t >= 2:
                    act.wait_ge(layer3_done, t - 1)
                nc.scalar.activation(h2[t % 2][:, 0, :], mlp_ps[0][:, 2, :], ACT.Relu,
                                     bias=b2_sb[:, 0:1]).then_inc(h2_by_act, 1)

            def copy_y(t):
                act.wait_ge(layer3_done, t + 1)
                nc.scalar.activation(y[:, P * t:P * (t + 1)], mlp_ps[0][0:1, 3, :], ACT.Copy).then_inc(y_ready, 1)

            for i in range(S):
                make_hi(i)
                if i >= 1:
                    copy_selected(i - 1)
                if i >= 2 and i - 2 < NG:
                    copy_group(0, i - 2)
            copy_selected(S - 1)
            for q in range(max(S - 2, 0), NG):
                copy_group(0, q)
            for t in range(T):
                copy_pairs(t, 0)
                if t == 0:
                    copy_group(1, 0)
                    copy_group(1, 1)
                else:
                    relu1(t - 1)
                copy_pairs(t, 1)
                if t > 0:
                    relu2(t - 1)
                    copy_y(t - 1)
                if t + 1 < T:
                    for q in range(2 if t == 0 else 0, NG):
                        copy_group(t + 1, q)
            relu1(T - 1)
            relu2(T - 1)
            copy_y(T - 1)

        @block.vector
        def _(dve):
            def make_lo(i):
                dve.wait_ge(hi_ready, i + 1)
                if i >= 2:
                    dve.wait_ge(onehot_used, CHUNKS * (i - 1))
                nc.vector.tensor_tensor(tab_lo[i % 2][:], tab[i % TB][:], tab_hi[i % 2][:].bitcast(f32),
                                        ALU.subtract).then_inc(lo_ready, 1)

            def make_onehots(i):
                dve.wait_ge(ids_bc_loaded[i % TB], 16 * (i // TB + 1))
                for c in range(CHUNKS):
                    o = CHUNKS * i + c
                    if o >= OB:
                        dve.wait_ge(onehot_used, o - OB + 1)
                    nc.vector.tensor_scalar(onehot[o % OB][:], ids_bc[i % TB][:], row_of[:, c:c + 1], None,
                                            ALU.is_equal).then_inc(onehot_ready, 1)

            def copy_group(t, q):
                n = NG * t + q
                if by_act(n):
                    return
                dve.wait_ge(transposed, n + 1)
                if q == 0:
                    if t >= 2:
                        dve.wait_ge(layer1_done, 2 * (t - 1))
                    nc.vector.tensor_copy(denseT[t % 2][:], tr_ps[n % 2][:, 0, :]).then_inc(dense_copied, 1)
                src, dst = feats_views(t, q)
                nc.vector.tensor_copy(dst, src).then_inc(feats_by_dve, 1)

            def copy_pairs(t, h):
                dve.wait_ge(gram_done, 2 * t + h + 1)
                if t >= 2:
                    dve.wait_ge(layer1_done, 2 * (t - 1))
                for s in (0, 1):
                    for j in range(Q):
                        src, dst = pairs_views(t, h, s, j)
                        last = nc.vector.tensor_copy(dst, src)
                last.then_inc(pairs_by_dve, 1)

            def relu1(t):
                if t == 0:
                    dve.wait_ge(small_loaded, 48)
                if t >= 2:
                    dve.wait_ge(layer2_done, C2 * (t - 1))
                dve.wait_ge(layer1_done, 2 * t + 2)
                for c in (2, 3):
                    last = nc.vector.tensor_scalar(h1[t % 2][:, c, :], mlp_ps[1][:, c - 2, :], b1_sb[:, c:c + 1],
                                                   0.0, ALU.add, ALU.max)
                last.then_inc(h1_by_dve, 1)

            def relu2(t):
                dve.wait_ge(layer2_done, C2 * t + 2)
                if t >= 2:
                    dve.wait_ge(layer3_done, t - 1)
                nc.vector.tensor_scalar(h2[t % 2][:, 1, :], mlp_ps[1][:, 2, :], b2_sb[:, 1:2], 0.0,
                                        ALU.add, ALU.max).then_inc(h2_by_dve, 1)

            nc.vector.memset(feats[:].rearrange("p t i s f -> p (t i s) f")[:, :, F:SLOT], 0.0)
            for i in range(2):
                last = nc.vector.memset(pairs[i][SLOT * 2:P, NK - 1, :], 0.0)
            last.then_inc(pads_ready, 1)
            dve.wait_ge(row_numbers, 1)
            nc.vector.tensor_copy(row_of[:], row_of_i[:]).then_inc(row_numbers, 1)
            dve.wait_ge(row_numbers, 2)
            for i in range(S):
                make_lo(i)
                make_onehots(i)
            for t in range(T):
                copy_pairs(t, 0)
                if t == 0:
                    copy_group(1, 0)
                    copy_group(1, 1)
                else:
                    relu1(t - 1)
                copy_pairs(t, 1)
                if t > 0:
                    relu2(t - 1)
                if t + 1 < T:
                    for q in range(2 if t == 0 else 0, NG):
                        copy_group(t + 1, q)
            relu1(T - 1)
            relu2(T - 1)


def kernel(**inputs):
    import numpy as np
    import concourse.bacc as bacc
    from concourse import mybir
    from concourse.bass_utils import run_bass_kernel_spmd as run

    P, F, Q = 128, N_TABLES + 1, 4
    nc = bacc.Bacc("TRN2", target_bir_lowering=False, num_devices=1)
    arrays = {}

    def give(name, a):
        a = np.ascontiguousarray(a)
        arrays[f"in_{name}"] = a
        return nc.dram_tensor(f"in_{name}", a.shape, mybir.dt.from_np(a.dtype), kind="ExternalInput").ap()

    ids = np.asarray(inputs["ids"])
    B = ids.shape[0]
    rows_of = [np.asarray(inputs[f"tbl_{n}"]).shape[0] for n in range(N_TABLES)]
    chosen = [n for n in range(N_TABLES) if rows_of[n] == min(rows_of)][:SELECTED]
    others = [n for n in range(N_TABLES) if n not in chosen]
    order = [n + 1 for n in chosen] + [0] + [n + 1 for n in others]
    ids_rows = give("ids_rows", ids[:, chosen].T)
    ids = give("ids", ids[:, others].reshape(B // P, P, len(others)).transpose(1, 0, 2))
    dense = give("dense", np.asarray(inputs["r_dense_features"]))
    sel_tables = [give(f"tbl_{n}", np.asarray(inputs[f"tbl_{n}"])) for n in chosen]
    tables = [give(f"tbl_{n}", np.asarray(inputs[f"tbl_{n}"])) for n in others]
    W1 = np.asarray(inputs["W_top1"])
    NK = -(-(F - 1) // Q)
    w1 = np.zeros((P, NK + 1, W1.shape[1]), W1.dtype)
    row = {pair: n for n, pair in enumerate((f, g) for f in range(F) for g in range(f + 1, F))}
    for f in range(F):
        for g in range(f + 1, F):
            pair = min(order[f], order[g]), max(order[f], order[g])
            w1[32 * ((g - 1) % Q) + f, (g - 1) // Q] = W1[row[pair]]
    w1[:, NK] = W1[len(row):]
    w1 = give("w1", w1)
    b1 = give("b1", np.asarray(inputs["b_top1"]).reshape(-1, P).T)
    w2 = give("w2", np.asarray(inputs["W_top2"]))
    b2 = give("b2", np.asarray(inputs["b_top2"]).reshape(-1, P).T)
    w3 = give("w3", np.asarray(inputs["W_top3"]).reshape(-1, P).T)
    out = nc.dram_tensor("out_0", (B, 1), mybir.dt.float32, kind="ExternalOutput").ap()
    dlrm_tower_kernel(nc, ids, ids_rows, dense, sel_tables, tables, w1, b1, w2, b2, w3, out.rearrange("b o -> o b"))
    r = run(nc, [arrays], core_ids=[0])
    return r.results[0]["out_0"]
```

```python
import concourse.bass as bass
from concourse import mybir
from contextlib import ExitStack

N_TABLES = 26
CHUNKS = 8
SELECTED = 7


def dlrm_tower_kernel(nc, ids, ids_rows, dense, sel_tables, tables, w1, w2, b2, w3, out):
    f32, f32r, i32 = mybir.dt.float32, mybir.dt.float32r, mybir.dt.int32
    ACT, ALU = mybir.ActivationFunctionType, mybir.AluOpType

    P = 128
    T = ids.shape[1]
    S = len(sel_tables)
    F = S + 1 + len(tables)
    M = F - S
    RP = sel_tables[0].shape[0] // CHUNKS
    G = F - 1
    Q = 4
    SLOT = 32
    SB = P // Q
    U = 4
    HB = SB // U
    NK = -(-G // Q)
    NG = -(-M // Q)
    H1, H2 = w1.shape[2], w2.shape[1]
    C1, C2 = H1 // P, H2 // P
    TB = 3
    OB = 8
    WS = 2
    WV = (NK + 1) // WS

    def group(q):
        return range(Q * q, min(Q * q + Q, M))

    with ExitStack() as ctx:
        def sb(name, shape, dt=f32):
            return ctx.enter_context(nc.sbuf_tensor(name, shape, dt))

        def ps(name, shape):
            return ctx.enter_context(nc.psum_tensor(name, shape, f32))

        def sem(name):
            return ctx.enter_context(nc.semaphore(name))

        ids_sb = sb("ids_sb", [P, T, M - 1], i32)
        ident = sb("ident", [P, P])
        rows = sb("rows", [P, T, M, P])
        feats = sb("feats", [P, T, SB, Q, SLOT])
        ids_bc = [sb(f"ids_bc{i}", [RP, T * P], i32) for i in range(TB)]
        stage = [sb(f"stage{i}", [P, CHUNKS * P]) for i in range(TB)]
        row_of_i = sb("row_of_i", [RP, CHUNKS], i32)
        row_of = sb("row_of", [RP, CHUNKS])
        pairs = [sb(f"pairs{i}", [P, NK + 1, P]) for i in range(2)]
        pairs_hi = [sb(f"pairs_hi{i}", [P, NK + 1, P], f32r) for i in range(2)]
        pairs_lo = [sb(f"pairs_lo{i}", [P, NK + 1, P], f32r) for i in range(2)]
        w1_hi = sb("w1_hi", [P, NK + 1, H1], f32r)
        w1_lo = sb("w1_lo", [P, NK + 1, H1], f32r)
        w2_sb = sb("w2_sb", [P, C1, H2])
        w3_sb = sb("w3_sb", [P, C2])
        b2_sb = sb("b2_sb", [P, C2])
        h1 = [sb(f"h1_{i}", [P, H1]) for i in range(2)]
        h1T = [sb(f"h1T_{i}", [P, C1, P]) for i in range(2)]
        h2T = [sb(f"h2T_{i}", [P, C2, P]) for i in range(2)]
        y = sb("y", [1, T * P])

        def tab_part(i, part):
            at = 4 * (i % 2) + 2 * part
            return w1_hi[0:RP, at:at + 2, :].rearrange("p a (b d) -> p (a b) d", d=P)

        def onehot(o):
            return w1_lo[0:RP, o % OB, :]

        tr_ps = [ps(f"tr_ps{i}", [P, Q, P]) for i in range(2)]
        gram_ps = [ps(f"gram_ps{i}", [P, HB, P]) for i in range(2)]
        l1_ps = ps("l1_ps", [P, H1])
        l2_ps = ps("l2_ps", [P, Q, P])

        ids_loaded = sem("ids_loaded")
        small_loaded = sem("small_loaded")
        w2_loaded = sem("w2_loaded")
        dense_loaded = sem("dense_loaded")
        ids_bc_loaded = [sem(f"ids_bc_loaded{i}") for i in range(TB)]
        stage_loaded = [sem(f"stage_loaded{i}") for i in range(TB)]
        gathered = [[sem(f"gathered{t}_{q}") for q in range(NG)] for t in range(T)]
        row_numbers = sem("row_numbers")
        hi_ready = sem("hi_ready")
        lo_ready = sem("lo_ready")
        onehot_ready = sem("onehot_ready")
        onehot_used = sem("onehot_used")
        selected_copied = sem("selected_copied")
        zeroed = sem("zeroed")
        ident_ready = sem("ident_ready")
        pads_zeroed = sem("pads_zeroed")
        pads_ready = sem("pads_ready")
        transposed = sem("transposed")
        turn_by_act = sem("turn_by_act")
        turn_by_dve = sem("turn_by_dve")
        dense_copied = sem("dense_copied")
        gram_done = sem("gram_done")
        pairs_by_act = sem("pairs_by_act")
        pairs_by_dve = sem("pairs_by_dve")
        pairs_hi_ready = sem("pairs_hi_ready")
        pairs_lo_ready = sem("pairs_lo_ready")
        layer1_done = sem("layer1_done")
        h1_ready = sem("h1_ready")
        layer2_done = sem("layer2_done")
        h2_ready = sem("h2_ready")
        layer3_done = sem("layer3_done")
        y_ready = sem("y_ready")
        stored = sem("stored")

        turns = [(t, q) for t in (0, 1) for q in range(NG)]
        for t in range(1, T - 1):
            turns += [(t + 1, 0), (t + 1, 1), (t - 1, None)] + [(t + 1, q) for q in range(2, NG)]
        turns += [(T - 2, None), (T - 1, None)]

        def by_act(n):
            return n < NG or n % 2 == 0

        def act_turns(n):
            return len([m for m in range(n) if by_act(m)])

        def dve_turns(n):
            return n - act_turns(n)

        block = ctx.enter_context(nc.Block())

        @block.sync
        def _(sp):
            w1_v = w1.rearrange("p (v k) n -> p v (k n)", k=WS)
            sp.dma_start(ids_sb[:], ids).then_inc(ids_loaded, 16)
            for i in range(S + WV):
                if i >= TB:
                    sp.wait_ge(lo_ready, i - TB + 1)
                if i < S:
                    if i >= TB:
                        sp.wait_ge(onehot_ready, CHUNKS * (i - TB + 1))
                    sp.dma_start(ids_bc[i % TB][:], ids_rows[i, :].partition_broadcast(RP)).then_inc(
                        ids_bc_loaded[i % TB], 16)
                    sp.dma_start(stage[i % TB][0:RP, :], sel_tables[i].rearrange("(p c) d -> p (c d)", c=CHUNKS)
                                 ).then_inc(stage_loaded[i % TB], 16)
                else:
                    sp.dma_start(stage[i % TB][:], w1_v[:, i - S, :]).then_inc(stage_loaded[i % TB], 16)
                if i == 0:
                    sp.dma_start(rows[:, :, 0, :], dense.rearrange("(t p) d -> p t d", p=P)).then_inc(
                        dense_loaded, 16)
            sp.dma_start(w2_sb[:], w2.rearrange("(c p) n -> p c n", p=P)).then_inc(w2_loaded, 16)
            sp.dma_start(b2_sb[:], b2).then_inc(small_loaded, 16)
            sp.dma_start(w3_sb[:], w3).then_inc(small_loaded, 16)
            sp.wait_ge(y_ready, T)
            sp.dma_start(out, y[:]).then_inc(stored, 16)
            sp.wait_ge(stored, 16)

        @block.gpsimd
        def _(pool):
            nc.gpsimd.memset(ident[:], 0.0).then_inc(zeroed, 1)
            pool.wait_ge(zeroed, 1)
            nc.gpsimd.affine_select(out=ident[:], in_=ident[:], compare_op=ALU.not_equal, fill=1.0, base=0,
                                    pattern=[[-1, P]], channel_multiplier=1).then_inc(ident_ready, 1)
            nc.gpsimd.iota(row_of_i[:], pattern=[[1, CHUNKS]], base=0, channel_multiplier=CHUNKS).then_inc(
                row_numbers, 1)
            pool.wait_ge(ids_loaded, 16)
            for t in range(T):
                for m in range(1, M):
                    nc.gpsimd.indirect_dma_start(
                        out=rows[:, t, m, :], out_offset=None, in_=tables[m - 1],
                        in_offset=bass.IndirectOffsetOnAxis(ap=ids_sb[:, t, m - 1:m], axis=0),
                    ).then_inc(gathered[t][m // Q], 16)

        @block.tensor
        def _(pe):
            def select(i):
                pe.wait_ge(hi_ready, i + 1)
                if i >= 2:
                    pe.wait_ge(selected_copied, i - 1)
                bank = gram_ps[i % 2][:, 0:T, :].rearrange("p a b -> p (a b)")
                steps = [(c, part) for c in range(CHUNKS) for part in (0, 1)]
                if i == 0:
                    steps.sort(key=lambda step: step[1])
                for n, (c, part) in enumerate(steps):
                    if part == 0:
                        pe.wait_ge(onehot_ready, CHUNKS * i + c + 1)
                    if part == 1 and c == 0:
                        pe.wait_ge(lo_ready, i + 1)
                    last = nc.tensor.matmul(bank, tab_part(i, part)[:, c, :], onehot(CHUNKS * i + c),
                                            start=(n == 0), stop=(n == len(steps) - 1))
                    if part == 1:
                        last.then_inc(onehot_used, 1)

            def free_turn(n):
                if n >= 2:
                    if turns[n - 2][1] == 0:
                        pe.wait_ge(dense_copied, turns[n - 2][0] + 1)
                    if by_act(n - 2):
                        pe.wait_ge(turn_by_act, act_turns(n - 1))
                    else:
                        pe.wait_ge(turn_by_dve, dve_turns(n - 1))

            def transpose_group(t, q):
                n = turns.index((t, q))
                if q == 0:
                    pe.wait_ge(dense_loaded, 16)
                pe.wait_ge(gathered[t][q], 16 * len([m for m in group(q) if m]))
                free_turn(n)
                for c, m in enumerate(group(q)):
                    last = nc.tensor.transpose(tr_ps[n % 2][:, c, :], rows[:, t, m, :], ident[:])
                last.then_inc(transposed, 1)

            def gram(t, h):
                u = U * t + h
                if u == 0:
                    pe.wait_ge(pads_ready, 1)
                    pe.wait_ge(selected_copied, S)
                if h == 0:
                    n = turns.index((t, NG - 1)) + 1
                    pe.wait_ge(turn_by_act, act_turns(n))
                    if t >= 1:
                        pe.wait_ge(turn_by_dve, dve_turns(n))
                if u >= 2:
                    pe.wait_ge(pairs_by_act, u - 1)
                    pe.wait_ge(pairs_by_dve, u - 1)
                for i in range(HB):
                    x = feats[:, t, HB * h + i, :, :]
                    last = nc.tensor.matmul(gram_ps[u % 2][:, i, 0:Q * G], x.rearrange("p s f -> p (s f)"),
                                            x[:, :, 1:F], start=True, stop=True)
                last.then_inc(gram_done, 1)

            def layer1(t):
                if t >= 1:
                    pe.wait_ge(h1_ready, t)
                pe.wait_ge(pairs_hi_ready, 2 * (t + 1))
                b = t % 2
                for k in range(NK + 1):
                    if t == 0 and k % WS == 0:
                        pe.wait_ge(lo_ready, S + k // WS + 1)
                    nc.tensor.matmul(l1_ps[:], pairs_hi[b][:, k, :], w1_hi[:, k, :], start=(k == 0), stop=False)
                    nc.tensor.matmul(l1_ps[:], pairs_hi[b][:, k, :], w1_lo[:, k, :], start=False, stop=False)
                pe.wait_ge(pairs_lo_ready, 2 * (t + 1))
                for k in range(NK + 1):
                    last = nc.tensor.matmul(l1_ps[:], pairs_lo[b][:, k, :], w1_hi[:, k, :], start=False,
                                            stop=(k == NK))
                last.then_inc(layer1_done, 1)

            def transpose_hidden(t):
                n = turns.index((t, None))
                pe.wait_ge(h1_ready, t + 1)
                free_turn(n)
                for c in range(C1):
                    last = nc.tensor.transpose(tr_ps[n % 2][:, c, :], h1[t % 2][:, P * c:P * (c + 1)], ident[:])
                last.then_inc(transposed, 1)

            def layer2(t):
                n = turns.index((t, None))
                if by_act(n):
                    pe.wait_ge(turn_by_act, act_turns(n + 1))
                else:
                    pe.wait_ge(turn_by_dve, dve_turns(n + 1))
                if t == 0:
                    pe.wait_ge(w2_loaded, 16)
                else:
                    pe.wait_ge(y_ready, t)
                for e in range(C2):
                    for c in range(C1):
                        last = nc.tensor.matmul(l2_ps[:, e, :], w2_sb[:, c, P * e:P * (e + 1)], h1T[t % 2][:, c, :],
                                                start=(c == 0), stop=(c == C1 - 1))
                last.then_inc(layer2_done, 1)

            def layer3(t):
                if t == 0:
                    pe.wait_ge(small_loaded, 32)
                pe.wait_ge(h2_ready, t + 1)
                for e in range(C2):
                    last = nc.tensor.matmul(l2_ps[0:1, C2, :], w3_sb[:, e:e + 1], h2T[t % 2][:, e, :],
                                            start=(e == 0), stop=(e == C2 - 1))
                last.then_inc(layer3_done, 1)

            pe.wait_ge(ident_ready, 1)
            for i in range(S):
                select(i)
                if 1 <= i <= NG:
                    transpose_group(0, i - 1)
            for q in range(S - 1, NG):
                transpose_group(0, q)
            gram(0, 0)
            gram(0, 1)
            for q in range(0, 2):
                transpose_group(1, q)
            gram(0, 2)
            gram(0, 3)
            for q in range(2, NG):
                transpose_group(1, q)
            for t in range(1, T):
                gram(t, 0)
                gram(t, 1)
                layer1(t - 1)
                if t + 1 < T:
                    transpose_group(t + 1, 0)
                    transpose_group(t + 1, 1)
                transpose_hidden(t - 1)
                gram(t, 2)
                gram(t, 3)
                layer2(t - 1)
                if t + 1 < T:
                    for q in range(2, NG):
                        transpose_group(t + 1, q)
                layer3(t - 1)
            layer1(T - 1)
            transpose_hidden(T - 1)
            layer2(T - 1)
            layer3(T - 1)

        def turn_views(t, q):
            n = turns.index((t, q))
            w = len(group(q))
            src = tr_ps[n % 2][:, 0:w, :].rearrange("p f (s i) -> p s i f", s=Q)
            dst = feats[:, t, :, :, S + Q * q:S + Q * q + w].rearrange("p i s f -> p s i f")
            return src, dst

        def pairs_views(t, h, s, j):
            nk = len(range(j, G, Q))
            src = gram_ps[h % 2][SLOT * s:SLOT * (s + 1), :, G * s + j:G * (s + 1):Q].rearrange("p i k -> p k i")
            dst = pairs[t % 2][SLOT * j:SLOT * (j + 1), 0:nk, SB * s + HB * h:SB * s + HB * (h + 1)]
            return src, dst

        def half(buffer, h):
            return buffer[:].rearrange("p k (s h i) -> p (k s) h i", s=Q, h=2)[:, :, h, :]

        @block.scalar
        def _(act):
            def make_hi(i):
                act.wait_ge(stage_loaded[i % TB], 16 * (i // TB + 1))
                if i >= S:
                    act.wait_ge(onehot_used, CHUNKS * S)
                    dst = w1_hi[:, WS * (i - S):WS * (i - S + 1), :].rearrange("p k n -> p (k n)")
                    nc.scalar.activation(dst, stage[i % TB][:], ACT.Copy).then_inc(hi_ready, 1)
                    return
                if i >= 2:
                    act.wait_ge(onehot_used, CHUNKS * (i - 1))
                src = stage[i % TB][0:RP, :].rearrange("p (c d) -> p c d", d=P)
                nc.scalar.activation(tab_part(i, 0), src, ACT.Copy).then_inc(hi_ready, 1)

            def copy_selected(i):
                act.wait_ge(onehot_used, CHUNKS * (i + 1))
                src = gram_ps[i % 2][:, 0:T, :].rearrange("p t (s i) -> p t s i", s=Q)
                dst = feats[:, :, :, :, i].rearrange("p t i s -> p t s i")
                nc.scalar.activation(dst, src, ACT.Copy).then_inc(selected_copied, 1)

            def copy_turn(t, q):
                n = turns.index((t, q))
                if not by_act(n):
                    return
                act.wait_ge(transposed, n + 1)
                if q is None:
                    if t >= 2:
                        act.wait_ge(layer2_done, t - 1)
                    nc.scalar.activation(h1T[t % 2][:], tr_ps[n % 2][:], ACT.Copy).then_inc(turn_by_act, 1)
                    return
                if q == 0:
                    if t >= 2:
                        act.wait_ge(pairs_lo_ready, 2 * (t - 1))
                    nc.scalar.activation(pairs[t % 2][:, NK, :], tr_ps[n % 2][:, 0, :], ACT.Copy).then_inc(
                        dense_copied, 1)
                src, dst = turn_views(t, q)
                nc.scalar.activation(dst, src, ACT.Copy).then_inc(turn_by_act, 1)

            def copy_pairs(t, h):
                act.wait_ge(gram_done, U * t + h + 1)
                if t >= 2:
                    act.wait_ge(pairs_lo_ready, 2 * (t - 1))
                for s in (2, 3):
                    for j in range(Q):
                        src, dst = pairs_views(t, h, s, j)
                        last = nc.scalar.activation(dst, src, ACT.Copy)
                last.then_inc(pairs_by_act, 1)

            def split_hi(t, h):
                act.wait_ge(pairs_by_act, U * t + 2 * (h + 1))
                act.wait_ge(pairs_by_dve, U * t + 2 * (h + 1))
                act.wait_ge(dense_copied, t + 1)
                if t == 0:
                    act.wait_ge(pads_ready, 1)
                if t >= 2:
                    act.wait_ge(layer1_done, t - 1)
                nc.scalar.activation(half(pairs_hi[t % 2], h), half(pairs[t % 2], h), ACT.Copy).then_inc(
                    pairs_hi_ready, 1)

            def relu1(t):
                act.wait_ge(layer1_done, t + 1)
                if t >= 2:
                    act.wait_ge(transposed, turns.index((t - 2, None)) + 1)
                nc.scalar.activation(h1[t % 2][:], l1_ps[:], ACT.Relu).then_inc(h1_ready, 1)

            def relu2(t):
                if t == 0:
                    act.wait_ge(small_loaded, 32)
                act.wait_ge(layer2_done, t + 1)
                if t >= 2:
                    act.wait_ge(layer3_done, t - 1)
                for e in range(C2):
                    last = nc.scalar.activation(h2T[t % 2][:, e, :], l2_ps[:, e, :], ACT.Relu, bias=b2_sb[:, e:e + 1])
                last.then_inc(h2_ready, 1)

            def copy_y(t):
                act.wait_ge(layer3_done, t + 1)
                nc.scalar.activation(y[:, P * t:P * (t + 1)], l2_ps[0:1, C2, :], ACT.Copy).then_inc(y_ready, 1)

            for i in range(S):
                make_hi(i)
                if i >= 1:
                    copy_selected(i - 1)
                if 2 <= i <= NG + 1:
                    copy_turn(0, i - 2)
            copy_selected(S - 1)
            for q in range(S - 2, NG):
                copy_turn(0, q)
            copy_pairs(0, 0)
            copy_pairs(0, 1)
            for q in range(0, 2):
                copy_turn(1, q)
            make_hi(S)
            copy_pairs(0, 2)
            copy_pairs(0, 3)
            for q in range(2, NG):
                copy_turn(1, q)
            split_hi(0, 0)
            split_hi(0, 1)
            for v in range(1, WV):
                make_hi(S + v)
            for t in range(1, T):
                copy_pairs(t, 0)
                copy_pairs(t, 1)
                split_hi(t, 0)
                relu1(t - 1)
                if t + 1 < T:
                    copy_turn(t + 1, 0)
                    copy_turn(t + 1, 1)
                copy_turn(t - 1, None)
                copy_pairs(t, 2)
                copy_pairs(t, 3)
                if t + 1 == T:
                    split_hi(t, 1)
                relu2(t - 1)
                if t + 1 < T:
                    for q in range(2, NG):
                        copy_turn(t + 1, q)
                copy_y(t - 1)
                if t + 1 < T:
                    split_hi(t, 1)
            relu1(T - 1)
            copy_turn(T - 1, None)
            relu2(T - 1)
            copy_y(T - 1)

        @block.vector
        def _(dve):
            def make_lo(i):
                dve.wait_ge(hi_ready, i + 1)
                if i >= S:
                    dve.wait_ge(onehot_used, CHUNKS * S)
                    at = WS * (i - S)
                    hi = w1_hi[:, at:at + WS, :].rearrange("p k n -> p (k n)")
                    lo = w1_lo[:, at:at + WS, :].rearrange("p k n -> p (k n)")
                    nc.vector.tensor_tensor(lo, stage[i % TB][:], hi.bitcast(f32), ALU.subtract).then_inc(lo_ready, 1)
                    return
                if i >= 2:
                    dve.wait_ge(onehot_used, CHUNKS * (i - 1))
                src = stage[i % TB][0:RP, :].rearrange("p (c d) -> p c d", d=P)
                nc.vector.tensor_tensor(tab_part(i, 1), src, tab_part(i, 0).bitcast(f32), ALU.subtract).then_inc(
                    lo_ready, 1)

            def make_onehots(i):
                dve.wait_ge(ids_bc_loaded[i % TB], 16 * (i // TB + 1))
                for c in range(CHUNKS):
                    o = CHUNKS * i + c
                    if o >= OB:
                        dve.wait_ge(onehot_used, o - OB + 1)
                    nc.vector.tensor_scalar(onehot(o), ids_bc[i % TB][:], row_of[:, c:c + 1], None,
                                            ALU.is_equal).then_inc(onehot_ready, 1)

            def copy_turn(t, q):
                n = turns.index((t, q))
                if by_act(n):
                    return
                dve.wait_ge(transposed, n + 1)
                if q is None:
                    if t >= 2:
                        dve.wait_ge(layer2_done, t - 1)
                    nc.vector.tensor_copy(h1T[t % 2][:], tr_ps[n % 2][:]).then_inc(turn_by_dve, 1)
                    return
                if q == 0:
                    if t >= 2:
                        dve.wait_ge(pairs_lo_ready, 2 * (t - 1))
                    nc.vector.tensor_copy(pairs[t % 2][:, NK, :], tr_ps[n % 2][:, 0, :]).then_inc(dense_copied, 1)
                src, dst = turn_views(t, q)
                nc.vector.tensor_copy(dst, src).then_inc(turn_by_dve, 1)

            def copy_pairs(t, h):
                dve.wait_ge(gram_done, U * t + h + 1)
                if t >= 2:
                    dve.wait_ge(pairs_lo_ready, 2 * (t - 1))
                for s in (0, 1):
                    for j in range(Q):
                        src, dst = pairs_views(t, h, s, j)
                        last = nc.vector.tensor_copy(dst, src)
                last.then_inc(pairs_by_dve, 1)

            def split_lo(t, h):
                dve.wait_ge(pairs_hi_ready, 2 * t + h + 1)
                if t >= 2:
                    dve.wait_ge(layer1_done, t - 1)
                nc.vector.tensor_tensor(half(pairs_lo[t % 2], h), half(pairs[t % 2], h),
                                        half(pairs_hi[t % 2], h).bitcast(f32), ALU.subtract).then_inc(
                    pairs_lo_ready, 1)

            dve.wait_ge(row_numbers, 1)
            nc.vector.tensor_copy(row_of[:], row_of_i[:]).then_inc(row_numbers, 1)
            nc.vector.memset(feats[:].rearrange("p t i s f -> p (t i s) f")[:, :, F:SLOT], 0.0)
            for i in range(2):
                last = nc.vector.memset(pairs[i][SLOT * 2:P, NK - 1, :], 0.0)
            last.then_inc(pads_zeroed, 1)
            dve.wait_ge(pads_zeroed, 1)
            for i in range(2):
                last = nc.vector.memset(pairs[i][SLOT * 2:SLOT * 2 + 1, NK - 1, :], 1.0)
            last.then_inc(pads_ready, 1)
            dve.wait_ge(row_numbers, 2)
            make_onehots(0)
            make_lo(0)
            for i in range(1, S):
                make_lo(i)
                make_onehots(i)
            copy_pairs(0, 0)
            copy_pairs(0, 1)
            for q in range(0, 2):
                copy_turn(1, q)
            make_lo(S)
            copy_pairs(0, 2)
            copy_pairs(0, 3)
            for q in range(2, NG):
                copy_turn(1, q)
            split_lo(0, 0)
            split_lo(0, 1)
            for v in range(1, WV):
                make_lo(S + v)
            for t in range(1, T):
                copy_pairs(t, 0)
                copy_pairs(t, 1)
                split_lo(t, 0)
                if t + 1 < T:
                    copy_turn(t + 1, 0)
                    copy_turn(t + 1, 1)
                copy_turn(t - 1, None)
                copy_pairs(t, 2)
                copy_pairs(t, 3)
                if t + 1 < T:
                    for q in range(2, NG):
                        copy_turn(t + 1, q)
                split_lo(t, 1)
            copy_turn(T - 1, None)


def kernel(**inputs):
    import numpy as np
    import concourse.bacc as bacc
    from concourse import mybir
    from concourse.bass_utils import run_bass_kernel_spmd as run

    P, F, Q = 128, N_TABLES + 1, 4
    nc = bacc.Bacc("TRN2", target_bir_lowering=False, num_devices=1)
    arrays = {}

    def give(name, a):
        a = np.ascontiguousarray(a)
        arrays[f"in_{name}"] = a
        return nc.dram_tensor(f"in_{name}", a.shape, mybir.dt.from_np(a.dtype), kind="ExternalInput").ap()

    ids = np.asarray(inputs["ids"])
    B = ids.shape[0]
    rows_of = [np.asarray(inputs[f"tbl_{n}"]).shape[0] for n in range(N_TABLES)]
    chosen = [n for n in range(N_TABLES) if rows_of[n] == min(rows_of)][:SELECTED]
    others = [n for n in range(N_TABLES) if n not in chosen]
    order = [n + 1 for n in chosen] + [0] + [n + 1 for n in others]
    ids_rows = give("ids_rows", ids[:, chosen].T)
    ids = give("ids", ids[:, others].reshape(B // P, P, len(others)).transpose(1, 0, 2))
    dense = give("dense", np.asarray(inputs["r_dense_features"]))
    sel_tables = [give(f"tbl_{n}", np.asarray(inputs[f"tbl_{n}"])) for n in chosen]
    tables = [give(f"tbl_{n}", np.asarray(inputs[f"tbl_{n}"])) for n in others]
    W1 = np.asarray(inputs["W_top1"])
    NK = -(-(F - 1) // Q)
    w1 = np.zeros((P, NK + 1, W1.shape[1]), W1.dtype)
    row = {pair: n for n, pair in enumerate((f, g) for f in range(F) for g in range(f + 1, F))}
    for f in range(F):
        for g in range(f + 1, F):
            pair = min(order[f], order[g]), max(order[f], order[g])
            w1[32 * ((g - 1) % Q) + f, (g - 1) // Q] = W1[row[pair]]
    w1[64, NK - 1] = np.asarray(inputs["b_top1"])
    w1[:, NK] = W1[len(row):]
    w1 = give("w1", w1)
    w2 = give("w2", np.asarray(inputs["W_top2"]))
    b2 = give("b2", np.asarray(inputs["b_top2"]).reshape(-1, P).T)
    w3 = give("w3", np.asarray(inputs["W_top3"]).reshape(-1, P).T)
    out = nc.dram_tensor("out_0", (B, 1), mybir.dt.float32, kind="ExternalOutput").ap()
    dlrm_tower_kernel(nc, ids, ids_rows, dense, sel_tables, tables, w1, w2, b2, w3, out.rearrange("b o -> o b"))
    r = run(nc, [arrays], core_ids=[0])
    return r.results[0]["out_0"]
```

```python
import concourse.bass as bass
from concourse import mybir
from contextlib import ExitStack

N_TABLES = 26
CHUNKS = 8
SELECTED = 8


def dlrm_tower_kernel(nc, ids, ids_rows, dense, sel_tables, tables, second, w1, w2, b2, w3, out):
    f32, f32r, i32 = mybir.dt.float32, mybir.dt.float32r, mybir.dt.int32
    ACT, ALU = mybir.ActivationFunctionType, mybir.AluOpType

    P = 128
    T = ids.shape[1]
    S = len(sel_tables)
    F = S + 1 + len(tables)
    M = len(tables)
    RP = sel_tables[0].shape[0] // CHUNKS
    R = F // 2
    Q = 4
    SLOT = 32
    SB = P // Q
    U = 4
    HB = SB // U
    NS = R + 1
    NK = -(-NS // Q)
    NG = -(-M // Q)
    H1, H2 = w1.shape[2], w2.shape[2]
    C1 = H1 // P
    TB = 3
    OB = 8
    WS = 2
    WARM = 18
    WV = -(-(NK + 1) // WS)

    def group(q):
        return range(Q * q, min(Q * q + Q, M))

    with ExitStack() as ctx:
        def sb(name, shape, dt=f32):
            return ctx.enter_context(nc.sbuf_tensor(name, shape, dt))

        def ps(name, shape):
            return ctx.enter_context(nc.psum_tensor(name, shape, f32))

        def sem(name):
            return ctx.enter_context(nc.semaphore(name))

        ids_sb = sb("ids_sb", [P, T, M], i32)
        ident = sb("ident", [P, P])
        rows = sb("rows", [P, T, M, P])
        feats = sb("feats", [P, T, SB, Q, SLOT])
        ids_bc = [sb(f"ids_bc{i}", [RP, T * P], i32) for i in range(TB)]
        tab_hi = [sb(f"tab_hi{i}", [P, CHUNKS, P], f32r) for i in range(2)]
        tab_lo = [sb(f"tab_lo{i}", [P, CHUNKS, P], f32r) for i in range(2)]
        onehots = sb("onehots", [RP, OB, T * P], f32r)
        stage = [sb(f"stage{i}", [P, CHUNKS * P]) for i in range(TB)]
        distance = sb("distance", [P, T * P])
        row_of_i = sb("row_of_i", [RP, CHUNKS], i32)
        row_of = sb("row_of", [RP, CHUNKS])
        dense_sb = sb("dense_sb", [P, T, P])
        dense_hi = sb("dense_hi", [P, T, P], f32r)
        dense_lo = sb("dense_lo", [P, T, P], f32r)
        pairs = [sb(f"pairs{i}", [P, NK, P]) for i in range(2)]
        pairs_hi = [sb(f"pairs_hi{i}", [P, NK, P], f32r) for i in range(2)]
        pairs_lo = [sb(f"pairs_lo{i}", [P, NK, P], f32r) for i in range(2)]
        w1_hi = sb("w1_hi", [P, NK + 1, H1], f32r)
        w1_lo = sb("w1_lo", [P, NK + 1, H1], f32r)
        w2_hi = sb("w2_hi", [P, C1, H2], f32r)
        w2_lo = sb("w2_lo", [P, C1, H2], f32r)
        w3_bc = sb("w3_bc", [P, H2])
        b2_sb = sb("b2_sb", [1, H2])
        b2_hi = sb("b2_hi", [1, H2], f32r)
        b2_lo = sb("b2_lo", [1, H2], f32r)
        ones = sb("ones", [1, P], f32r)
        h1 = [distance, sb("h1_1", [P, H1])]
        h1T_hi = [tab_hi[i][:, 0:C1, :] for i in range(2)]
        h1T_lo = [tab_lo[i][:, 0:C1, :] for i in range(2)]
        h2w3 = sb("h2w3", [P, H2])
        y = sb("y", [P, T])
        second_sb = sb("second_sb", [P, Q, NK], i32)

        def tab_part(i, part):
            return (tab_lo if part else tab_hi)[i % 2][0:RP, :, :]

        def onehot(o):
            return onehots[:, o % OB, :]

        tr_ps = [ps(f"tr_ps{i}", [P, Q, P]) for i in range(2)]
        gram_ps = [ps(f"gram_ps{i}", [P, HB, P]) for i in range(2)]
        l1_ps = ps("l1_ps", [P, H1])
        l2_ps = ps("l2_ps", [P, H1])
        HH, CH = H1 // 2, C1 // 2

        def l1_half(e):
            return l1_ps[:, 0:HH] if e == 0 else gram_ps[0][:, 0:CH, :].rearrange("p a b -> p (a b)")

        ids_loaded = sem("ids_loaded")
        small_loaded = sem("small_loaded")
        dense_loaded = sem("dense_loaded")
        second_loaded = sem("second_loaded")
        ids_bc_loaded = [sem(f"ids_bc_loaded{i}") for i in range(TB)]
        stage_loaded = [sem(f"stage_loaded{i}") for i in range(TB)]
        gathered = [[sem(f"gathered{t}_{q}") for q in range(NG)] for t in range(T)]
        half_loaded = sem("half_loaded")
        half_hi_ready = sem("half_hi_ready")
        row_numbers = sem("row_numbers")
        hi_ready = sem("hi_ready")
        lo_ready = sem("lo_ready")
        onehot_by_dve = sem("onehot_by_dve")
        distance_ready = sem("distance_ready")
        onehot_by_act = sem("onehot_by_act")
        onehot_used = sem("onehot_used")
        selected_copied = sem("selected_copied")
        zeroed = sem("zeroed")
        ident_ready = sem("ident_ready")
        pads_zeroed = sem("pads_zeroed")
        pads_ready = sem("pads_ready")
        feats_padded = sem("feats_padded")
        transposed = sem("transposed")
        turn_by_act = sem("turn_by_act")
        turn_by_dve = sem("turn_by_dve")
        dense_copied = sem("dense_copied")
        dense_hi_ready = sem("dense_hi_ready")
        dense_lo_ready = sem("dense_lo_ready")
        bias_hi_ready = sem("bias_hi_ready")
        bias_ready = sem("bias_ready")
        ones_ready = sem("ones_ready")
        gram_done = sem("gram_done")
        pairs_by_act = sem("pairs_by_act")
        pairs_by_dve = sem("pairs_by_dve")
        pairs_hi_ready = sem("pairs_hi_ready")
        pairs_lo_ready = sem("pairs_lo_ready")
        layer1_done = sem("layer1_done")
        h1_ready = sem("h1_ready")
        layer2_done = sem("layer2_done")
        h1T_hi_ready = sem("h1T_hi_ready")
        y_ready = sem("y_ready")
        stored = sem("stored")

        turns = [(t, q) for t in (0, 1) for q in range(NG)]
        turns += [(2, 0), (0, None)] + [(2, q) for q in range(1, NG)]
        for t in range(2, T - 1):
            turns += [(t - 1, None)] + [(t + 1, q) for q in range(NG)]
        turns += [(T - 2, None), (T - 1, 0, None), (T - 1, 1, None)]

        def by_act(n):
            return n < 2 * NG or (n % 2 == 0 and turns[n][-1] is not None)

        def act_turns(n):
            return len([m for m in range(n) if by_act(m)])

        def dve_turns(n):
            return n - act_turns(n)

        def piece(i):
            return slice(WS * (i - S), min(WS * (i - S + 1), NK + 1))

        block = ctx.enter_context(nc.Block())

        @block.sync
        def _(sp):
            sp.dma_start(ids_sb[:], ids).then_inc(ids_loaded, 16)
            for i in range(S + WV + 1):
                if i >= TB:
                    sp.wait_ge(lo_ready, i - TB + 1)
                if i < S:
                    if i >= TB:
                        sp.wait_ge(onehot_by_dve, (CHUNKS - 1) * (i - TB + 1))
                        sp.wait_ge(onehot_by_act, i - TB + 1)
                    sp.dma_start(ids_bc[i % TB][:], ids_rows[i, :].partition_broadcast(RP)).then_inc(
                        ids_bc_loaded[i % TB], 16)
                    src = sel_tables[i].rearrange("(p c) d -> p (c d)", c=CHUNKS)
                    if i == 0:
                        half_row = CHUNKS * P // 2
                        sp.dma_start(stage[0][0:RP, 0:half_row], src[:, 0:half_row]).then_inc(half_loaded, 16)
                        sp.dma_start(stage[0][0:RP, half_row:], src[:, half_row:]).then_inc(stage_loaded[0], 16)
                    else:
                        sp.dma_start(stage[i % TB][0:RP, :], src).then_inc(stage_loaded[i % TB], 16)
                else:
                    src = w1[:, piece(i), :] if i < S + WV else w2
                    src = src.rearrange("p c n -> p (c n)")
                    sp.dma_start(stage[i % TB][:, 0:src.shape[1]], src).then_inc(stage_loaded[i % TB], 16)
                if i == 1:
                    sp.dma_start(dense_sb[:].rearrange("d t p -> d (t p)"), dense).then_inc(dense_loaded, 16)
                    sp.dma_start(second_sb[:], second).then_inc(second_loaded, 16)
            sp.dma_start(b2_sb[:], b2).then_inc(small_loaded, 16)
            sp.dma_start(w3_bc[:], w3[0, :].partition_broadcast(P)).then_inc(small_loaded, 16)
            with nc.allow_non_contiguous_dma(reason="one sum a partition"):
                sp.wait_ge(y_ready, T - 1)
                sp.dma_start(out[:, 0:T - 1], y[:, 0:T - 1]).then_inc(stored, 16)
                sp.wait_ge(y_ready, T)
                sp.dma_start(out[:, T - 1:T], y[:, T - 1:T]).then_inc(stored, 16)
            sp.wait_ge(stored, 32)

        @block.gpsimd
        def _(pool):
            nc.gpsimd.memset(ident[:], 0.0).then_inc(zeroed, 1)
            pool.wait_ge(zeroed, 1)
            nc.gpsimd.affine_select(out=ident[:], in_=ident[:], compare_op=ALU.not_equal, fill=1.0, base=0,
                                    pattern=[[-1, P]], channel_multiplier=1).then_inc(ident_ready, 1)
            nc.gpsimd.iota(row_of_i[:], pattern=[[1, CHUNKS]], base=0, channel_multiplier=CHUNKS).then_inc(
                row_numbers, 1)
            pool.wait_ge(ids_loaded, 16)
            for t in range(T):
                for m in range(M):
                    nc.gpsimd.indirect_dma_start(
                        out=rows[:, t, m, :], out_offset=None, in_=tables[m],
                        in_offset=bass.IndirectOffsetOnAxis(ap=ids_sb[:, t, m:m + 1], axis=0),
                    ).then_inc(gathered[t][m // Q], 16)

        @block.tensor
        def _(pe):
            def warm_up():
                for _ in range(WARM):
                    nc.tensor.transpose(l1_ps[:, 0:P], ident[:], ident[:])

            def select(i):
                if i == 0:
                    pe.wait_ge(half_hi_ready, 1)
                else:
                    pe.wait_ge(hi_ready, i + 1)
                if i >= 2:
                    pe.wait_ge(selected_copied, i - 1)
                bank = gram_ps[i % 2][:, 0:T, :].rearrange("p a b -> p (a b)")
                steps = [(c, part) for c in range(CHUNKS) for part in (0, 1)]
                if i == 0:
                    steps.sort(key=lambda step: step[1])
                for n, (c, part) in enumerate(steps):
                    if i == 0 and part == 0 and c == CHUNKS // 2:
                        pe.wait_ge(hi_ready, 1)
                    if part == 0 and c < CHUNKS - 1:
                        pe.wait_ge(onehot_by_dve, (CHUNKS - 1) * i + c + 1)
                    if part == 0 and c == CHUNKS - 1:
                        pe.wait_ge(onehot_by_act, i + 1)
                    if part == 1 and c == 0:
                        pe.wait_ge(lo_ready, i + 1)
                    last = nc.tensor.matmul(bank, tab_part(i, part)[:, c, :], onehot(CHUNKS * i + c),
                                            start=(n == 0), stop=(n == len(steps) - 1))
                    if part == 1:
                        last.then_inc(onehot_used, 1)

            def free_turn(n):
                if n >= 2:
                    if by_act(n - 2):
                        pe.wait_ge(turn_by_act, act_turns(n - 1))
                    else:
                        pe.wait_ge(turn_by_dve, dve_turns(n - 1))

            def transpose_group(t, q):
                n = turns.index((t, q))
                pe.wait_ge(gathered[t][q], 16 * len(group(q)))
                free_turn(n)
                for c, m in enumerate(group(q)):
                    last = nc.tensor.transpose(tr_ps[n % 2][:, c, :], rows[:, t, m, :], ident[:])
                last.then_inc(transposed, 1)

            def gram(t, h):
                u = U * t + h
                if u == 0:
                    pe.wait_ge(feats_padded, 1)
                    pe.wait_ge(selected_copied, S)
                    pe.wait_ge(dense_copied, 1)
                if h == 0:
                    n = turns.index((t, NG - 1)) + 1
                    pe.wait_ge(turn_by_act, act_turns(n))
                    if t >= 2:
                        pe.wait_ge(turn_by_dve, dve_turns(n))
                if u >= 2:
                    pe.wait_ge(pairs_by_dve, u - 1)
                for i in range(HB):
                    x = feats[:, t, HB * h + i, :, :]
                    last = nc.tensor.matmul(gram_ps[u % 2][:, i, 0:Q * F], x.rearrange("p s f -> p (s f)"),
                                            x[:, :, 0:F], start=True, stop=True)
                last.then_inc(gram_done, 1)

            def dense_products(t, acc, cols):
                nc.tensor.matmul(acc, dense_hi[:, t, :], w1_hi[:, 0, cols], start=True, stop=False)
                nc.tensor.matmul(acc, dense_hi[:, t, :], w1_lo[:, 0, cols], start=False, stop=False)
                nc.tensor.matmul(acc, dense_lo[:, t, :], w1_hi[:, 0, cols], start=False, stop=False)

            def layer1(t, on_the_way=()):
                if t >= 1:
                    pe.wait_ge(h1_ready, t)
                b = t % 2
                if t == 0:
                    pe.wait_ge(dense_lo_ready, 1)
                for k in range(NK + 1):
                    if t == 0 and k % WS == 0:
                        pe.wait_ge(lo_ready, S + k // WS + 1)
                    if k == 0:
                        dense_products(t, l1_ps[:], slice(0, H1))
                        continue
                    if k == 1:
                        pe.wait_ge(pairs_hi_ready, 2 * (t + 1))
                    x = pairs_hi[b][:, k - 1, :]
                    nc.tensor.matmul(l1_ps[:], x, w1_hi[:, k, :], start=False, stop=False)
                    nc.tensor.matmul(l1_ps[:], x, w1_lo[:, k, :], start=False, stop=False)
                pe.wait_ge(pairs_lo_ready, 2 * (t + 1))
                for k in range(1, NK + 1):
                    if k == 1 + NK // 2:
                        for q in on_the_way:
                            transpose_group(t + 1, q)
                    last = nc.tensor.matmul(l1_ps[:], pairs_lo[b][:, k - 1, :], w1_hi[:, k, :], start=False,
                                            stop=(k == NK))
                last.then_inc(layer1_done, 1)

            def transpose_hidden(t):
                n = turns.index((t, None))
                pe.wait_ge(h1_ready, t + 1)
                free_turn(n)
                for c in range(C1):
                    last = nc.tensor.transpose(tr_ps[n % 2][:, c, :], h1[t % 2][:, P * c:P * (c + 1)], ident[:])
                last.then_inc(transposed, 1)

            def layer2_start(t):
                if t == 0:
                    pe.wait_ge(bias_ready, 1)
                    pe.wait_ge(ones_ready, 1)
                    pe.wait_ge(lo_ready, S + WV + 1)
                else:
                    pe.wait_ge(y_ready, t)
                nc.tensor.matmul(l2_ps[:, 0:H2], ones[:], b2_hi[:], start=True, stop=False)
                nc.tensor.matmul(l2_ps[:, 0:H2], ones[:], b2_lo[:], start=False, stop=False)

            def layer2_hi(t, pieces=range(C1)):
                b, first = t % 2, pieces[0] == 0
                pe.wait_ge(h1T_hi_ready, t + (1 if first else 2))
                for c in pieces:
                    nc.tensor.matmul(l2_ps[:, 0:H2], h1T_hi[b][:, c, :], w2_hi[:, c, :], start=False, stop=False)
                    nc.tensor.matmul(l2_ps[:, 0:H2], h1T_hi[b][:, c, :], w2_lo[:, c, :], start=False, stop=False)

            def layer2_lo(t, pieces=range(C1)):
                b, first, final = t % 2, pieces[0] == 0, pieces[-1] == C1 - 1
                n = turns.index((t, None) if t < T - 1 else (t, 0 if first else 1, None))
                pe.wait_ge(turn_by_dve, dve_turns(n + 1))
                for c in pieces:
                    last = nc.tensor.matmul(l2_ps[:, 0:H2], h1T_lo[b][:, c, :], w2_hi[:, c, :], start=False,
                                            stop=(c == C1 - 1))
                if final:
                    last.then_inc(layer2_done, 1)

            def layer2(t):
                layer2_start(t)
                layer2_hi(t)
                layer2_lo(t)

            def last_layer1(e):
                b = (T - 1) % 2
                cols = [slice(HH * i, HH * (i + 1)) for i in (0, 1)]
                if e == 0:
                    pe.wait_ge(h1_ready, T - 1)
                    dense_products(T - 1, l1_half(0), cols[0])
                    pe.wait_ge(pairs_by_dve, U * T - 1)
                    dense_products(T - 1, l1_half(1), cols[1])
                    pe.wait_ge(pairs_hi_ready, 2 * T + 1)
                for k in range(1, NK + 1):
                    x = pairs_hi[b][:, k - 1, :]
                    nc.tensor.matmul(l1_half(e), x, w1_hi[:, k, cols[e]], start=False, stop=False)
                    nc.tensor.matmul(l1_half(e), x, w1_lo[:, k, cols[e]], start=False, stop=False)
                pe.wait_ge(pairs_lo_ready, 2 * T + 1)
                if e == 1:
                    last_transpose_hidden(0)
                for k in range(1, NK + 1):
                    last = nc.tensor.matmul(l1_half(e), pairs_lo[b][:, k - 1, :], w1_hi[:, k, cols[e]],
                                            start=False, stop=(k == NK))
                last.then_inc(layer1_done, 1)

            def last_transpose_hidden(e):
                n = turns.index((T - 1, e, None))
                pe.wait_ge(h1_ready, T + e)
                free_turn(n)
                for c in range(CH):
                    at = HH * e + P * c
                    last = nc.tensor.transpose(tr_ps[n % 2][:, c, :], h1[(T - 1) % 2][:, at:at + P], ident[:])
                last.then_inc(transposed, 1)

            pe.wait_ge(ident_ready, 1)
            warm_up()
            for i in range(S):
                select(i)
                if 1 <= i <= NG:
                    transpose_group(0, i - 1)
            for q in range(S - 1, NG):
                transpose_group(0, q)
            transpose_group(1, 0)
            transpose_group(1, 1)
            gram(0, 0)
            gram(0, 1)
            transpose_group(1, 2)
            gram(0, 2)
            for q in range(3, NG):
                transpose_group(1, q)
            gram(0, 3)
            gram(1, 0)
            gram(1, 1)
            layer1(0)
            transpose_group(2, 0)
            gram(1, 2)
            transpose_hidden(0)
            gram(1, 3)
            transpose_group(2, 1)
            layer2(0)
            transpose_group(2, 2)
            layer1(1, range(3, NG))
            for t in range(2, T - 1):
                gram(t, 0)
                transpose_hidden(t - 1)
                gram(t, 1)
                transpose_group(t + 1, 0)
                gram(t, 2)
                gram(t, 3)
                transpose_group(t + 1, 1)
                layer2(t - 1)
                transpose_group(t + 1, 2)
                layer1(t, range(3, NG - 1) if t == T - 2 else range(3, NG))
            transpose_group(T - 1, NG - 1)
            transpose_hidden(T - 2)
            gram(T - 1, 0)
            gram(T - 1, 1)
            gram(T - 1, 2)
            gram(T - 1, 3)
            layer2(T - 2)
            last_layer1(0)
            last_layer1(1)
            layer2_start(T - 1)
            layer2_hi(T - 1, range(0, CH))
            last_transpose_hidden(1)
            layer2_lo(T - 1, range(0, CH))
            layer2_hi(T - 1, range(CH, C1))
            layer2_lo(T - 1, range(CH, C1))

        def turn_views(t, q):
            n = turns.index((t, q))
            w = len(group(q))
            src = tr_ps[n % 2][:, 0:w, :].rearrange("p f (s i) -> p s i f", s=Q)
            dst = feats[:, t, :, :, S + 1 + Q * q:S + 1 + Q * q + w].rearrange("p i s f -> p s i f")
            return src, dst

        def pairs_views(t, h, s, j, which):
            nk = len(range(j, NS, Q))
            at = F * s + j + R * which
            src = gram_ps[h % 2][SLOT * s:SLOT * (s + 1), :, at:at + Q * (nk - 1) + 1:Q].rearrange("p i k -> p k i")
            dst = pairs[t % 2][SLOT * j:SLOT * (j + 1), 0:nk, SB * s + HB * h:SB * s + HB * (h + 1)]
            return src, dst

        def half(buffer, h):
            return buffer[:].rearrange("p k (s h i) -> p (k s) h i", s=Q, h=2)[:, :, h, :]

        def quarter(buffer, h):
            return buffer[:].rearrange("p k (s h i) -> p (k s) h i", s=Q, h=U)[:, :, h, :]

        @block.scalar
        def _(act):
            def make_hi(i):
                act.wait_ge(stage_loaded[i % TB], 16 * (i // TB + 1))
                if i == S + WV:
                    nc.scalar.activation(w2_hi[:].rearrange("p c n -> p (c n)"), stage[i % TB][:],
                                         ACT.Copy).then_inc(hi_ready, 1)
                    return
                if i >= S:
                    dst = w1_hi[:, piece(i), :].rearrange("p k n -> p (k n)")
                    nc.scalar.activation(dst, stage[i % TB][:, 0:dst.shape[1]], ACT.Copy).then_inc(hi_ready, 1)
                    return
                if i >= 2:
                    act.wait_ge(onehot_used, CHUNKS * (i - 1))
                src = stage[i % TB][0:RP, :].rearrange("p (c d) -> p c d", d=P)
                first = CHUNKS // 2 if i == 0 else 0
                nc.scalar.activation(tab_part(i, 0)[:, first:, :], src[:, first:, :], ACT.Copy).then_inc(hi_ready, 1)

            def make_first_half_hi():
                act.wait_ge(half_loaded, 16)
                src = stage[0][0:RP, :].rearrange("p (c d) -> p c d", d=P)
                nc.scalar.activation(tab_part(0, 0)[:, 0:CHUNKS // 2, :], src[:, 0:CHUNKS // 2, :],
                                     ACT.Copy).then_inc(half_hi_ready, 1)

            def make_last_onehot(i):
                if i == 0:
                    act.wait_ge(row_numbers, 2)
                else:
                    act.wait_ge(onehot_by_act, i)
                act.wait_ge(ids_bc_loaded[i % TB], 16 * (i // TB + 1))
                nc.scalar.activation(distance[0:RP, :], ids_bc[i % TB][:], ACT.Abs, scale=-1.0,
                                     bias=row_of[:, CHUNKS - 1:CHUNKS]).then_inc(distance_ready, 1)
                act.wait_ge(distance_ready, i + 1)
                if i >= 1:
                    act.wait_ge(onehot_used, CHUNKS * i)
                nc.scalar.activation(onehot(CHUNKS * i + CHUNKS - 1), distance[0:RP, :], ACT.Relu, scale=-1.0,
                                     bias=1.0).then_inc(onehot_by_act, 1)

            def copy_selected(i):
                act.wait_ge(onehot_used, CHUNKS * (i + 1))
                src = gram_ps[i % 2][:, 0:T, :].rearrange("p t (s i) -> p t s i", s=Q)
                dst = feats[:, :, :, :, i].rearrange("p t i s -> p t s i")
                nc.scalar.activation(dst, src, ACT.Copy).then_inc(selected_copied, 1)

            def hidden_hi(t, e=None):
                n = turns.index((t, None) if e is None else (t, e, None))
                pieces = slice(0, C1) if e is None else slice(CH * e, CH * (e + 1))
                act.wait_ge(transposed, n + 1)
                if t >= 2:
                    act.wait_ge(layer2_done, t - 1)
                dst = h1T_hi[t % 2][:, pieces, :]
                nc.scalar.activation(dst, tr_ps[n % 2][:, 0:dst.shape[1], :], ACT.Copy).then_inc(h1T_hi_ready, 1)

            def copy_turn(t, q):
                n = turns.index((t, q))
                if not by_act(n):
                    return
                act.wait_ge(transposed, n + 1)
                src, dst = turn_views(t, q)
                nc.scalar.activation(dst, src, ACT.Copy).then_inc(turn_by_act, 1)

            def copy_pairs(t, h):
                act.wait_ge(gram_done, U * t + h + 1)
                if t >= 2:
                    act.wait_ge(pairs_lo_ready, 2 * (t - 1))
                for s in range(Q):
                    for j in range(Q):
                        src, dst = pairs_views(t, h, s, j, 0)
                        last = nc.scalar.activation(dst, src, ACT.Copy)
                    last.then_inc(pairs_by_act, 1)

            def split_hi(t, h):
                act.wait_ge(pairs_by_dve, U * t + 2 * (h + 1))
                if t == 0:
                    act.wait_ge(pads_ready, 1)
                if t >= 2:
                    act.wait_ge(layer1_done, t - 1)
                nc.scalar.activation(half(pairs_hi[t % 2], h), half(pairs[t % 2], h), ACT.Copy).then_inc(
                    pairs_hi_ready, 1)

            def last_split_hi(h):
                act.wait_ge(pairs_by_dve, U * (T - 1) + h + 1)
                b = (T - 1) % 2
                nc.scalar.activation(quarter(pairs_hi[b], h), quarter(pairs[b], h), ACT.Copy).then_inc(
                    pairs_hi_ready, 1)

            def copy_dense():
                act.wait_ge(dense_loaded, 16)
                nc.scalar.activation(feats[:, :, :, :, S].rearrange("p t i s -> p t s i"),
                                     dense_sb[:].rearrange("p t (s i) -> p t s i", s=Q), ACT.Copy).then_inc(
                    dense_copied, 1)
                nc.scalar.activation(dense_hi[:], dense_sb[:], ACT.Copy).then_inc(dense_hi_ready, 1)

            def prepare_bias():
                act.wait_ge(small_loaded, 32)
                nc.scalar.activation(b2_hi[:], b2_sb[:], ACT.Copy).then_inc(bias_hi_ready, 1)
                nc.scalar.activation(ones[:], ident[0:1, :], ACT.Relu, scale=0.0, bias=1.0).then_inc(ones_ready, 1)

            def relu1(t):
                act.wait_ge(layer1_done, t + 1)
                if t >= 2:
                    act.wait_ge(transposed, turns.index((t - 2, None)) + 1)
                nc.scalar.activation(h1[t % 2][:], l1_ps[:], ACT.Relu).then_inc(h1_ready, 1)

            def last_relu1(e):
                act.wait_ge(layer1_done, T + e)
                if e == 0:
                    act.wait_ge(transposed, turns.index((T - 3, None)) + 1)
                nc.scalar.activation(h1[(T - 1) % 2][:, HH * e:HH * (e + 1)], l1_half(e), ACT.Relu).then_inc(
                    h1_ready, 1)

            act.wait_ge(ident_ready, 1)
            pad = feats[:].rearrange("p t i s f -> p (t i s) f")[:, :, F:SLOT]
            nc.scalar.activation(pad, ident[:, 0:1].unsqueeze(2).to_broadcast(list(pad.shape)), ACT.Copy,
                                 scale=0.0).then_inc(feats_padded, 1)
            make_first_half_hi()
            make_hi(0)
            make_last_onehot(0)
            make_hi(1)
            for i in range(1, S):
                if i + 1 < S:
                    make_hi(i + 1)
                make_last_onehot(i)
                copy_selected(i - 1)
                if 2 <= i <= NG + 1:
                    copy_turn(0, i - 2)
            copy_dense()
            make_hi(S)
            copy_selected(S - 1)
            for q in range(S - 2, NG):
                copy_turn(0, q)
            copy_turn(1, 0)
            copy_turn(1, 1)
            copy_pairs(0, 0)
            copy_pairs(0, 1)
            copy_turn(1, 2)
            make_hi(S + 1)
            copy_pairs(0, 2)
            for q in range(3, NG):
                copy_turn(1, q)
            copy_pairs(0, 3)
            split_hi(0, 0)
            split_hi(0, 1)
            copy_pairs(1, 0)
            make_hi(S + 2)
            copy_pairs(1, 1)
            for v in range(3, WV + 1):
                make_hi(S + v)
            prepare_bias()
            split_hi(1, 0)
            relu1(0)
            copy_turn(2, 0)
            copy_pairs(1, 2)
            hidden_hi(0)
            copy_pairs(1, 3)
            split_hi(1, 1)
            for q in range(1, NG):
                copy_turn(2, q)
            relu1(1)
            for t in range(2, T - 1):
                copy_pairs(t, 0)
                hidden_hi(t - 1)
                copy_pairs(t, 1)
                split_hi(t, 0)
                copy_turn(t + 1, 0)
                copy_pairs(t, 2)
                copy_pairs(t, 3)
                copy_turn(t + 1, 1)
                split_hi(t, 1)
                for q in range(2, NG):
                    copy_turn(t + 1, q)
                relu1(t)
            copy_pairs(T - 1, 0)
            hidden_hi(T - 2)
            copy_pairs(T - 1, 1)
            copy_pairs(T - 1, 2)
            split_hi(T - 1, 0)
            copy_pairs(T - 1, 3)
            last_split_hi(2)
            last_split_hi(3)
            last_relu1(0)
            hidden_hi(T - 1, 0)
            last_relu1(1)
            hidden_hi(T - 1, 1)

        @block.vector
        def _(dve):
            def make_lo(i):
                dve.wait_ge(hi_ready, i + 1)
                if i == S + WV:
                    nc.vector.tensor_tensor(w2_lo[:].rearrange("p c n -> p (c n)"), stage[i % TB][:],
                                            w2_hi[:].rearrange("p c n -> p (c n)").bitcast(f32),
                                            ALU.subtract).then_inc(lo_ready, 1)
                    return
                if i >= S:
                    hi = w1_hi[:, piece(i), :].rearrange("p k n -> p (k n)")
                    lo = w1_lo[:, piece(i), :].rearrange("p k n -> p (k n)")
                    nc.vector.tensor_tensor(lo, stage[i % TB][:, 0:hi.shape[1]], hi.bitcast(f32), ALU.subtract).then_inc(lo_ready, 1)
                    return
                if i >= 2:
                    dve.wait_ge(onehot_used, CHUNKS * (i - 1))
                src = stage[i % TB][0:RP, :].rearrange("p (c d) -> p c d", d=P)
                nc.vector.tensor_tensor(tab_part(i, 1), src, tab_part(i, 0).bitcast(f32), ALU.subtract).then_inc(
                    lo_ready, 1)

            def make_onehots(i):
                dve.wait_ge(ids_bc_loaded[i % TB], 16 * (i // TB + 1))
                for c in range(CHUNKS - 1):
                    o = CHUNKS * i + c
                    if o >= OB:
                        dve.wait_ge(onehot_used, o - OB + 1)
                    nc.vector.tensor_scalar(onehot(o), ids_bc[i % TB][:], row_of[:, c:c + 1], None,
                                            ALU.is_equal).then_inc(onehot_by_dve, 1)

            def copy_turn(t, q):
                n = turns.index((t, q))
                if by_act(n):
                    return
                dve.wait_ge(transposed, n + 1)
                src, dst = turn_views(t, q)
                nc.vector.tensor_copy(dst, src).then_inc(turn_by_dve, 1)

            def copy_pairs(t, h):
                if t + h == 0:
                    dve.wait_ge(second_loaded, 16)
                for s in range(Q):
                    dve.wait_ge(pairs_by_act, Q * (U * t + h) + s + 1)
                    for j in range(Q):
                        src, dst = pairs_views(t, h, s, j, 1)
                        at = second_sb[SLOT * s:SLOT * (s + 1), j, 0:src.shape[1]]
                        last = nc.vector.copy_predicated(
                            dst, at.unsqueeze(2).to_broadcast(list(src.shape)), src)
                last.then_inc(pairs_by_dve, 1)

            def split_lo(t, h):
                dve.wait_ge(pairs_hi_ready, 2 * t + h + 1)
                if t >= 2:
                    dve.wait_ge(layer1_done, t - 1)
                nc.vector.tensor_tensor(half(pairs_lo[t % 2], h), half(pairs[t % 2], h),
                                        half(pairs_hi[t % 2], h).bitcast(f32), ALU.subtract).then_inc(
                    pairs_lo_ready, 1)

            def last_split_lo(h):
                dve.wait_ge(pairs_hi_ready, 2 * (T - 1) + h)
                b = (T - 1) % 2
                nc.vector.tensor_tensor(quarter(pairs_lo[b], h), quarter(pairs[b], h),
                                        quarter(pairs_hi[b], h).bitcast(f32), ALU.subtract).then_inc(
                    pairs_lo_ready, 1)

            def hidden_lo(t, e=None):
                n = turns.index((t, None) if e is None else (t, e, None))
                pieces = slice(0, C1) if e is None else slice(CH * e, CH * (e + 1))
                dve.wait_ge(h1T_hi_ready, t + 1 + (e or 0))
                if t >= 2:
                    dve.wait_ge(layer2_done, t - 1)
                dst, hi = h1T_lo[t % 2][:, pieces, :], h1T_hi[t % 2][:, pieces, :]
                nc.vector.tensor_tensor(dst, tr_ps[n % 2][:, 0:dst.shape[1], :], hi.bitcast(f32),
                                        ALU.subtract).then_inc(turn_by_dve, 1)

            def finish(t):
                if t == 0:
                    dve.wait_ge(small_loaded, 32)
                else:
                    dve.wait_ge(y_ready, t)
                dve.wait_ge(layer2_done, t + 1)
                nc.vector.scalar_tensor_tensor(h2w3[:], l2_ps[:, 0:H2], 0.0, w3_bc[:], ALU.max, ALU.mult,
                                               accum_out=y[:, t:t + 1]).then_inc(y_ready, 1)

            dve.wait_ge(row_numbers, 1)
            nc.vector.tensor_copy(row_of[:], row_of_i[:]).then_inc(row_numbers, 1)
            for i in range(2):
                last = nc.vector.memset(pairs[i][SLOT * 2:P, NK - 1, :], 0.0)
            last.then_inc(pads_zeroed, 1)
            dve.wait_ge(pads_zeroed, 1)
            for i in range(2):
                last = nc.vector.memset(pairs[i][SLOT * 2:SLOT * 2 + 1, NK - 1, :], 1.0)
            last.then_inc(pads_ready, 1)
            dve.wait_ge(row_numbers, 2)
            make_onehots(0)
            make_lo(0)
            for i in range(1, S):
                make_lo(i)
                make_onehots(i)
            copy_turn(1, 0)
            copy_turn(1, 1)
            dve.wait_ge(dense_hi_ready, 1)
            nc.vector.tensor_tensor(dense_lo[:], dense_sb[:], dense_hi[:].bitcast(f32), ALU.subtract).then_inc(
                dense_lo_ready, 1)
            make_lo(S)
            copy_pairs(0, 0)
            copy_pairs(0, 1)
            copy_turn(1, 2)
            copy_pairs(0, 2)
            for q in range(3, NG):
                copy_turn(1, q)
            copy_pairs(0, 3)
            make_lo(S + 1)
            copy_pairs(1, 0)
            make_lo(S + 2)
            split_lo(0, 0)
            split_lo(0, 1)
            copy_pairs(1, 1)
            split_lo(1, 0)
            for v in range(3, WV + 1):
                make_lo(S + v)
            dve.wait_ge(bias_hi_ready, 1)
            nc.vector.tensor_tensor(b2_lo[:], b2_sb[:], b2_hi[:].bitcast(f32), ALU.subtract).then_inc(bias_ready, 1)
            copy_turn(2, 0)
            copy_pairs(1, 2)
            hidden_lo(0)
            copy_pairs(1, 3)
            split_lo(1, 1)
            for q in range(1, NG - 1):
                copy_turn(2, q)
            finish(0)
            copy_turn(2, NG - 1)
            for t in range(2, T - 1):
                copy_pairs(t, 0)
                copy_pairs(t, 1)
                hidden_lo(t - 1)
                copy_turn(t + 1, 0)
                copy_pairs(t, 2)
                copy_pairs(t, 3)
                split_lo(t, 0)
                copy_turn(t + 1, 1)
                split_lo(t, 1)
                finish(t - 1)
                for q in range(2, NG):
                    copy_turn(t + 1, q)
            copy_pairs(T - 1, 0)
            copy_pairs(T - 1, 1)
            hidden_lo(T - 2)
            copy_pairs(T - 1, 2)
            copy_pairs(T - 1, 3)
            split_lo(T - 1, 0)
            last_split_lo(2)
            last_split_lo(3)
            finish(T - 2)
            hidden_lo(T - 1, 0)
            hidden_lo(T - 1, 1)
            finish(T - 1)


def kernel(**inputs):
    import numpy as np
    import concourse.bacc as bacc
    from concourse import mybir
    from concourse.bass_utils import run_bass_kernel_spmd as run

    P, F, Q = 128, N_TABLES + 1, 4
    nc = bacc.Bacc("TRN2", target_bir_lowering=False, num_devices=1)
    arrays = {}

    def give(name, a):
        a = np.ascontiguousarray(a)
        arrays[f"in_{name}"] = a
        return nc.dram_tensor(f"in_{name}", a.shape, mybir.dt.from_np(a.dtype), kind="ExternalInput").ap()

    ids = np.asarray(inputs["ids"])
    B = ids.shape[0]
    rows_of = [np.asarray(inputs[f"tbl_{n}"]).shape[0] for n in range(N_TABLES)]
    chosen = [n for n in range(N_TABLES) if rows_of[n] == min(rows_of)][:SELECTED]
    others = [n for n in range(N_TABLES) if n not in chosen]
    order = [n + 1 for n in chosen] + [0] + [n + 1 for n in others]
    ids_rows = give("ids_rows", ids[:, chosen].T)
    ids = give("ids", ids[:, others].reshape(B // P, P, len(others)).transpose(1, 0, 2))
    dense = give("dense", np.asarray(inputs["r_dense_features"]).T)
    sel_tables = [give(f"tbl_{n}", np.asarray(inputs[f"tbl_{n}"])) for n in chosen]
    tables = [give(f"tbl_{n}", np.asarray(inputs[f"tbl_{n}"])) for n in others]
    W1 = np.asarray(inputs["W_top1"])
    R = F // 2
    NK = -(-(R + 1) // Q)
    w1 = np.zeros((P, NK + 1, W1.shape[1]), W1.dtype)
    second = np.zeros((Q, 32, Q, NK), np.int32)
    row = {pair: n for n, pair in enumerate((f, g) for f in range(F) for g in range(f + 1, F))}
    left = dict(row)
    for g in range(R + 1):
        for f in range(F):
            second[:, f, g % Q, g // Q] = (f - g) % F > R
            other = g + R if (f - g) % F > R else g
            pair = tuple(sorted((order[f], order[other])))
            if pair in left:
                w1[32 * (g % Q) + f, 1 + g // Q] = W1[left.pop(pair)]
    assert not left
    second = give("second", second.reshape(P, Q, NK))
    w1[64, NK] = np.asarray(inputs["b_top1"])
    w1[:, 0] = W1[len(row):]
    w1 = give("w1", w1)
    W2 = np.asarray(inputs["W_top2"])
    w2 = give("w2", W2.reshape(-1, P, W2.shape[1]).transpose(1, 0, 2))
    b2 = give("b2", np.asarray(inputs["b_top2"]).reshape(1, -1))
    w3 = give("w3", np.asarray(inputs["W_top3"]).reshape(1, -1))
    out = nc.dram_tensor("out_0", (B, 1), mybir.dt.float32, kind="ExternalOutput").ap()
    dlrm_tower_kernel(nc, ids, ids_rows, dense, sel_tables, tables, second, w1, w2, b2, w3,
                      out.rearrange("(t p) o -> p (t o)", p=P))
    r = run(nc, [arrays], core_ids=[0])
    return r.results[0]["out_0"]
```
